# Optimizing a Trainium2 kernel written in Bass

```python
import numpy as np
import jax
import jax.numpy as jnp

def _softmax(x, axis=-1):
    return jax.nn.softmax(x, axis=axis)

def _gelu(x):
    return jax.nn.gelu(x, approximate=True)

def _silu(x):
    return jax.nn.silu(x)

def _sigmoid(x):
    return jax.nn.sigmoid(x)

def _layernorm(x, axis=-1, eps=1e-05):
    m = jnp.mean(x, axis=axis, keepdims=True)
    v = jnp.var(x, axis=axis, keepdims=True)
    return (x - m) / jnp.sqrt(v + eps)

def _scatter_add(tgt, idx, src, axis=0):
    return tgt.at[idx].add(src)

def _segment_sum(src, seg, n):
    return jax.ops.segment_sum(src, seg, n)
kernel_name = 'mk_adaln_d1_jaxref_r8_5ae1de'

def setup_inputs(seed: int=0):
    np.random.seed(seed)
    _w = jnp.asarray

    def _L0_attn_setup():
        import jax, jax.numpy as jnp
        import numpy as np
        B, S, H, NH = (8, 512, 128, 16)
        HD = H // NH
        EPS_ATTN = 1e-06
        EPS_LN = 1e-12
        key = jax.random.key(seed)
        ks = jax.random.split(key, 10)
        s = 1.0 / np.sqrt(H)
        return {'input_tensor': jax.random.normal(ks[0], (B, S, H), dtype=jnp.float32), 'attention_mask': jnp.zeros((B, S), dtype=jnp.int32), 'Wq': jax.random.normal(ks[1], (H, H), dtype=jnp.float32) * s, 'bq': jnp.zeros((H,), dtype=jnp.float32), 'Wk': jax.random.normal(ks[2], (H, H), dtype=jnp.float32) * s, 'bk': jnp.zeros((H,), dtype=jnp.float32), 'Wv': jax.random.normal(ks[3], (H, H), dtype=jnp.float32) * s, 'bv': jnp.zeros((H,), dtype=jnp.float32), 'Wd': jax.random.normal(ks[4], (H, H), dtype=jnp.float32) * s, 'bd': jnp.zeros((H,), dtype=jnp.float32), 'gamma': jnp.ones((H,), dtype=jnp.float32), 'beta': jnp.zeros((H,), dtype=jnp.float32)}
    _L0_attn_in = _L0_attn_setup()

    def _L0_ffn_setup():
        import jax, jax.numpy as jnp
        import numpy as np
        D_MODEL = 128
        EXPANSION = 4
        D_HIDDEN = D_MODEL * EXPANSION
        NUM_STAGES = int(np.log2(D_HIDDEN))

        def butterfly(y, weights, dim):
            lead = y.shape[:-1]
            for stage in range(weights.shape[0]):
                s = 2 ** stage
                nb = dim // (2 * s)
                yr = y.reshape(*lead, nb, 2, s)
                a = yr[..., 0, :]
                b = yr[..., 1, :]
                w = weights[stage].reshape(nb, s, 2, 2)
                na = w[..., 0, 0] * a + w[..., 0, 1] * b
                nb2 = w[..., 1, 0] * a + w[..., 1, 1] * b
                y = jnp.stack([na, nb2], axis=-2).reshape(*lead, dim)
            return y
        key = jax.random.key(seed)
        ks = jax.random.split(key, 6)
        B, S = (4, 256)
        x = jax.random.normal(ks[0], (B, S, D_MODEL), jnp.float32)
        W_exp = jax.random.normal(ks[1], (D_MODEL, D_HIDDEN), jnp.float32) * 0.02
        b_exp = jnp.zeros((D_HIDDEN,), jnp.float32)
        up_weights = jax.random.normal(ks[2], (NUM_STAGES, D_HIDDEN // 2, 2, 2), jnp.float32) * 0.02
        up_bias = jnp.zeros((D_HIDDEN,), jnp.float32)
        down_weights = jax.random.normal(ks[3], (NUM_STAGES, D_HIDDEN // 2, 2, 2), jnp.float32) * 0.02
        W_con = jax.random.normal(ks[4], (D_HIDDEN, D_MODEL), jnp.float32) * 0.02
        b_con = jnp.zeros((D_MODEL,), jnp.float32)
        down_bias = jnp.zeros((D_MODEL,), jnp.float32)
        return dict(x=x, W_exp=W_exp, b_exp=b_exp, up_weights=up_weights, up_bias=up_bias, down_weights=down_weights, W_con=W_con, b_con=b_con, down_bias=down_bias)
    _L0_ffn_in = _L0_ffn_setup()
    _L0_c = _w((lambda *s: np.random.randn(*s).astype(np.float32) * 0.05)(4, 128))
    _L0_wmod = _w((lambda *s: np.random.randn(*s).astype(np.float32) * 0.05)(128, 6 * 128) * 128 ** (-0.5))
    _d = {'L0_attn_input_tensor': _L0_attn_in['input_tensor'], 'L0_attn_attention_mask': _L0_attn_in['attention_mask'], 'L0_attn_Wq': _L0_attn_in['Wq'], 'L0_attn_bq': _L0_attn_in['bq'], 'L0_attn_Wk': _L0_attn_in['Wk'], 'L0_attn_bk': _L0_attn_in['bk'], 'L0_attn_Wv': _L0_attn_in['Wv'], 'L0_attn_bv': _L0_attn_in['bv'], 'L0_attn_Wd': _L0_attn_in['Wd'], 'L0_attn_bd': _L0_attn_in['bd'], 'L0_attn_gamma': _L0_attn_in['gamma'], 'L0_attn_beta': _L0_attn_in['beta'], 'L0_ffn_W_exp': _L0_ffn_in['W_exp'], 'L0_ffn_b_exp': _L0_ffn_in['b_exp'], 'L0_ffn_up_weights': _L0_ffn_in['up_weights'], 'L0_ffn_up_bias': _L0_ffn_in['up_bias'], 'L0_ffn_down_weights': _L0_ffn_in['down_weights'], 'L0_ffn_W_con': _L0_ffn_in['W_con'], 'L0_ffn_b_con': _L0_ffn_in['b_con'], 'L0_ffn_down_bias': _L0_ffn_in['down_bias'], 'L0_c': _L0_c, 'L0_wmod': _L0_wmod}
    _x0 = _d['L0_attn_input_tensor']
    _d['L0_attn_input_tensor'] = jax.random.normal(jax.random.fold_in(jax.random.key(seed), 1), (4, 1024, 128), dtype=_x0.dtype)
    del _x0
    return _d

def reference(L0_attn_input_tensor, L0_attn_attention_mask, L0_attn_Wq, L0_attn_bq, L0_attn_Wk, L0_attn_bk, L0_attn_Wv, L0_attn_bv, L0_attn_Wd, L0_attn_bd, L0_attn_gamma, L0_attn_beta, L0_ffn_W_exp, L0_ffn_b_exp, L0_ffn_up_weights, L0_ffn_up_bias, L0_ffn_down_weights, L0_ffn_W_con, L0_ffn_b_con, L0_ffn_down_bias, L0_c, L0_wmod):

    def _L0_attn_ref(input_tensor, attention_mask, Wq, bq, Wk, bk, Wv, bv, Wd, bd, gamma, beta):
        import jax, jax.numpy as jnp
        import numpy as np
        B, S, H, NH = (8, 512, 128, 16)
        HD = H // NH
        EPS_ATTN = 1e-06
        EPS_LN = 1e-12
        x = input_tensor
        b, s, h = x.shape
        q = (x @ Wq.T + bq).reshape(b, s, NH, HD)
        k = (x @ Wk.T + bk).reshape(b, s, NH, HD)
        v = (x @ Wv.T + bv).reshape(b, s, NH, HD)
        q = jax.nn.elu(q) + 1.0
        k = jax.nn.elu(k) + 1.0
        kv = jnp.einsum('nshd,nshm->nhmd', k, v)
        z = 1.0 / jnp.einsum('nlhd,nhd->nlh', q, k.sum(axis=1) + EPS_ATTN)
        ctx = jnp.einsum('nlhd,nhmd,nlh->nlhm', q, kv, z).reshape(b, s, h)
        hs = ctx @ Wd.T + bd
        hs = hs + x
        mu = hs.mean(axis=-1, keepdims=True)
        var = ((hs - mu) ** 2).mean(axis=-1, keepdims=True)
        out = (hs - mu) / jnp.sqrt(var + EPS_LN) * gamma + beta
        return out

    def _L0_ffn_ref(x, W_exp, b_exp, up_weights, up_bias, down_weights, W_con, b_con, down_bias):
        import jax, jax.numpy as jnp
        import numpy as np
        D_MODEL = 128
        EXPANSION = 4
        D_HIDDEN = D_MODEL * EXPANSION
        NUM_STAGES = int(np.log2(D_HIDDEN))

        def butterfly(y, weights, dim):
            lead = y.shape[:-1]
            for stage in range(weights.shape[0]):
                s = 2 ** stage
                nb = dim // (2 * s)
                yr = y.reshape(*lead, nb, 2, s)
                a = yr[..., 0, :]
                b = yr[..., 1, :]
                w = weights[stage].reshape(nb, s, 2, 2)
                na = w[..., 0, 0] * a + w[..., 0, 1] * b
                nb2 = w[..., 1, 0] * a + w[..., 1, 1] * b
                y = jnp.stack([na, nb2], axis=-2).reshape(*lead, dim)
            return y
        h = jnp.einsum('bsd,dh->bsh', x, W_exp) + b_exp
        h = butterfly(h, up_weights, D_HIDDEN)
        h = jax.nn.gelu(h + up_bias, approximate=False)
        h = butterfly(h, down_weights, D_HIDDEN)
        y = jnp.einsum('bsh,hd->bsd', h, W_con) + b_con
        return y + down_bias
    x = L0_attn_input_tensor
    mod = (_silu(L0_c) @ L0_wmod).reshape(L0_c.shape[0], 6, 1, -1)
    sa, ca, ga, sb, cb, gb = (mod[:, 0], mod[:, 1], mod[:, 2], mod[:, 3], mod[:, 4], mod[:, 5])
    ga = (2 * (ga >= 0) - 1) * jnp.maximum(jnp.abs(ga), 0.25)
    gb = (2 * (gb >= 0) - 1) * jnp.maximum(jnp.abs(gb), 0.25)
    h = _layernorm(x, axis=-1) * (1 + ca) + sa
    x = x + ga * _L0_attn_ref(h, L0_attn_attention_mask, L0_attn_Wq, L0_attn_bq, L0_attn_Wk, L0_attn_bk, L0_attn_Wv, L0_attn_bv, L0_attn_Wd, L0_attn_bd, L0_attn_gamma, L0_attn_beta)
    h = _layernorm(x, axis=-1) * (1 + cb) + sb
    x = x + gb * _L0_ffn_ref(h, L0_ffn_W_exp, L0_ffn_b_exp, L0_ffn_up_weights, L0_ffn_up_bias, L0_ffn_down_weights, L0_ffn_W_con, L0_ffn_b_con, L0_ffn_down_bias)
    return x

_drawn_inputs = setup_inputs


def setup_inputs(seed=0):
    import zlib

    import numpy as np

    out = dict(_drawn_inputs(seed))
    spreads = {'L0_attn_bq': (0.0, 0.8),
     'L0_attn_bk': (0.0, 0.8),
     'L0_attn_bv': (0.0, 0.344),
     'L0_attn_bd': (0.0, 0.339),
     'L0_attn_gamma': (1.0, 0.2),
     'L0_attn_beta': (0.0, 0.374),
     'L0_ffn_b_exp': (0.0, 0.1),
     'L0_ffn_up_bias': (0.0, 0.1),
     'L0_ffn_b_con': (0.0, 0.368),
     'L0_ffn_down_bias': (0.0, 0.305)}
    factors = {'L0_attn_Wq': 8.0, 'L0_attn_Wk': 8.0, 'L0_attn_Wv': 5.55}
    for name, (base, spread) in spreads.items():
        noise = np.random.default_rng([zlib.crc32(name.encode()), seed]).standard_normal(out[name].shape)
        drawn = base * np.exp(spread * noise) if base else spread * noise
        out[name] = jnp.asarray(drawn.astype(out[name].dtype))
    for name, factor in factors.items():
        out[name] = (out[name] * factor).astype(out[name].dtype)
    return out
```

```python
from contextlib import ExitStack

import concourse.bass as bass
from concourse import mybir

ALU = mybir.AluOpType
ACT = mybir.ActivationFunctionType
AX_X = mybir.AxisListType.X
F32 = mybir.dt.float32
BF16 = mybir.dt.bfloat16

P = 128
TILES = 4
LN_EPS = 1e-5
ATTN_LN_EPS = 1e-12
ATTN_EPS = 1e-6
GATE_FLOOR = 0.25


def adaln_block_kernel(nc, x_in, Wq, bq, Wk, bk, Wv, bv, Wd, bd, gamma, beta, W_exp, b_exp, up_w, up_bias,
                       down_w, W_con, b_con, down_bias, c_in, wmod, out):
    B, S, D = x_in.shape
    HID = W_exp.shape[1]
    CH = HID // P
    NS = up_w.shape[0]
    HEADS, HD = 16, D // 16
    GROUPS = B * S // (TILES * P)
    PER_B = GROUPS // B
    assert D == P and PER_B == 2 and CH == 4 and NS == 9 and GROUPS == 8
    SMALL = NS - 2

    x_v = x_in.rearrange("b (p j) d -> p b j d", p=P)
    out_v = out.rearrange("b (p j) d -> p b j d", p=P)

    with ExitStack() as ctx:
        def sb(name, shape, dt=F32):
            return ctx.enter_context(nc.sbuf_tensor(name, shape, dt))

        def sem(name):
            return ctx.enter_context(nc.semaphore(name))

        bank = [ctx.enter_context(nc.psum_tensor(f"bank{i}", [P, 512], F32)) for i in range(8)]

        x = sb("x", [P, B * 8, D])
        q = sb("q", [P, B * 8, D])
        r = sb("r", [P, B * 8, D + 1])
        mv1 = sb("mv1", [P, 8, 2])
        rs1 = sb("rs1", [P, B * 8])
        nb1 = sb("nb1", [P, B * 8])
        ve1 = sb("ve1", [P, 8])
        nm1 = sb("nm1", [P, 8])
        ident = sb("ident", [P, P])
        ones = sb("ones", [P, P])
        ones_bf = sb("ones_bf", [P, P], BF16)
        head_mask = sb("head_mask", [P, P])
        sel = sb("sel", [P // 2, SMALL, 2, P])
        power = sb("power", [P, 8])
        eps1 = sb("eps1", [P, 8])
        eps23 = sb("eps23", [P, 8])
        rows = sb("rows", [P, P])
        cols = sb("cols", [P, 15])
        w_raw = sb("w_raw", [P, 4, P])
        wT = sb("wT", [P, 4, P])
        wmod_s = sb("wmod_s", [P, 6 * D])
        bias_in = sb("bias_in", [3, 2 * D])
        bias_b = sb("bias_b", [3, 2 * D], BF16)
        bias_r = sb("bias_r", [3, 2 * D])
        bias_b2 = sb("bias_b2", [3, 2 * D], BF16)
        bias_r2 = sb("bias_r2", [3, 2 * D])
        bias_m = sb("bias_m", [3, 2 * D])
        bias_m2 = sb("bias_m2", [3, 2 * D])
        bias3 = sb("bias3", [P, 2 * D], BF16)
        bv_row = sb("bv_row", [1, D])
        vb_row = sb("vb_row", [1, D])
        bd_rep = sb("bd_rep", [P, D])
        gamma_rep = sb("gamma_rep", [P, D])
        beta_rep = sb("beta_rep", [P, D])
        sig = sb("sig", [P, 3, 4])
        sc = sb("sc", [P, 4])
        sc_rep = sb("sc_rep", [P, B, P])
        modc = sb("modc", [P, 6, B])
        gbw = sb("gbw", [P, 3, B])
        gbc = sb("gbc", [P, 2, B])
        bsum = sb("bsum", [P, 1])
        scale_rep = sb("scale_rep", [P, B, D])
        shift_rep = sb("shift_rep", [P, B, D])
        ga_rep = sb("ga_rep", [P, B, D])
        ga_sign = sb("ga_sign", [P, B, D])
        ga_abs = sb("ga_abs", [P, B, D])
        gg_rep = sb("gg_rep", [P, B, D])
        gbeta_rep = sb("gbeta_rep", [P, B, D])
        act = sb("act", [P, 2, CH, TILES * P])
        raw_small = [act[0:P // 2, i, :, :].rearrange("p c n -> p (c n)") for i in range(2)]
        raw_big = [sb(f"raw_big{i}", [P, 2048]) for i in range(2)]
        t_down = raw_big[0][:, :].rearrange("p (c n) -> p c n", c=CH)
        prod = [sb(f"prod{i}", [P, 8 * (2 ** SMALL - 1) + 1032]) for i in range(2)]
        h3T = prod[0][:, 0:1024].rearrange("p (k n) -> p k n", k=2)
        yT = prod[0][:, 1024:2048].rearrange("p (k n) -> p k n", k=2)
        t_mat = [sb(f"t_mat{i}", [P, CH, HID]) for i in range(2)]
        wexp_s = sb("wexp_s", [P, HID])
        wexpT = sb("wexpT", [P, CH, D])
        wcon_s = sb("wcon_s", [P, CH, D])
        w_up = sb("w_up", [P, HID])
        w_down = sb("w_down", [P, CH, D])
        b_up = sb("b_up", [P, CH])
        bn1 = sb("bn1", [P, 2, TILES, 6])
        n1 = sb("n1", [P, 2, TILES, D])
        hT = sb("hT", [P, 2, TILES * P])
        e = sb("e", [P, 2, 512])
        ev = sb("ev", [P, 2, 512])
        kf = sb("kf", [P, 2, TILES, D])
        gs = sb("gs", [P, B, D + 1])
        gT = sb("gT", [P, B, D])
        ks_row = sb("ks_row", [1, B, D])
        ks_eps = sb("ks_eps", [P, B])
        ks_diag = sb("ks_diag", [P, B, D])
        ks_rep = sb("ks_rep", [P, B, D])
        kvT = sb("kvT", [P, B, D])
        m_mat = sb("m_mat", [P, B, D])
        qn, qT, n3 = n1, hT, kf
        qk = sb("qk", [P, TILES, D])
        den = sb("den", [P, TILES * HEADS])
        z = sb("z", [P, TILES * HEADS])
        hs = e[:, :, :].rearrange("p k (t d) -> p k t d", d=D)
        bn2 = sb("bn2", [P, TILES, 6])
        bn3 = sb("bn3", [P, TILES, 6])
        mv = sb("mv", [P, 2, 8, 2])
        ve = sb("ve", [P, 8])
        nm = sb("nm", [P, 8])
        rs = sb("rs", [P, 2, 8])
        nb = sb("nb", [P, 2, 8])
        nh = sb("nh", [P, 2, TILES, D])

        rows_in = sem("rows_in")
        rows_clear = sem("rows_clear")
        w_in = sem("w_in")
        bias_ld = sem("bias_ld")
        wmod_in = sem("wmod_in")
        reps_in = sem("reps_in")
        bv_in = sem("bv_in")
        x_ld = [sem(f"x_ld{g}") for g in range(GROUPS)]
        small_in = [sem(f"small_in{i}") for i in range(2)]
        big_in = [sem(f"big_in{i}") for i in range(2)]
        ffn_in = sem("ffn_in")
        stored = sem("stored")
        const_ready = sem("const_ready")
        power_ready = sem("power_ready")
        sel_zero = sem("sel_zero")
        sel_ready = sem("sel_ready")
        id_zero = sem("id_zero")
        id_ready = sem("id_ready")
        mask_step = sem("mask_step")
        cols_ready = sem("cols_ready")
        cols_copied = sem("cols_copied")
        wT_ready = sem("wT_ready")
        wT_copied = sem("wT_copied")
        silu_exp = sem("silu_exp")
        silu_step = sem("silu_step")
        sc_ready = sem("sc_ready")
        sc_rep_ready = sem("sc_rep_ready")
        modT_ready = sem("modT_ready")
        modc_step = sem("modc_step")
        modc_ready = sem("modc_ready")
        mod_rep = sem("mod_rep")
        rep_copied = sem("rep_copied")
        ga_copied = sem("ga_copied")
        gate_step = sem("gate_step")
        gate_ready = sem("gate_ready")
        bias_step = sem("bias_step")
        bias_ready = sem("bias_ready")
        vb_mm = sem("vb_mm")
        vb_ready = sem("vb_ready")
        factors_ready = sem("factors_ready")
        prod_step = [sem(f"prod_step{i}") for i in range(2)]
        bn1_done = sem("bn1_done")
        ln1_stats = sem("ln1_stats")
        ln1_pool = sem("ln1_pool")
        ln1_scale = sem("ln1_scale")
        n1_ready = sem("n1_ready")
        r_half = sem("r_half")
        r_ready = sem("r_ready")
        n1T_ready = sem("n1T_ready")
        hT_ready = sem("hT_ready")
        qk_ready = sem("qk_ready")
        relu_ready = sem("relu_ready")
        exp_ready = sem("exp_ready")
        phi_ready = sem("phi_ready")
        g_done = sem("g_done")
        g_saved = sem("g_saved")
        gT_mm = sem("gT_mm")
        gT_saved = sem("gT_saved")
        ks_mm = sem("ks_mm")
        ks_saved = sem("ks_saved")
        ks_eps_ready = sem("ks_eps_ready")
        ks_diag_ready = sem("ks_diag_ready")
        ksrep_mm = sem("ksrep_mm")
        ksrep_saved = sem("ksrep_saved")
        kv_mm = sem("kv_mm")
        kv_saved = sem("kv_saved")
        m_mm = sem("m_mm")
        m_saved = sem("m_saved")
        wexpT_mm = sem("wexpT_mm")
        wexpT_saved = sem("wexpT_saved")
        wup_mm = sem("wup_mm")
        wup_saved = sem("wup_saved")
        bup_mm = sem("bup_mm")
        bup_saved = sem("bup_saved")
        td_mm = sem("td_mm")
        td_saved = sem("td_saved")
        wdown_mm = sem("wdown_mm")
        wdown_saved = sem("wdown_saved")
        qks_ready = sem("qks_ready")
        den_ready = sem("den_ready")
        z_ready = sem("z_ready")
        qn_ready = sem("qn_ready")
        qnT_mm = sem("qnT_mm")
        qT_ready = sem("qT_ready")
        attn_mm = sem("attn_mm")
        hs_ready = sem("hs_ready")
        bn2_done = sem("bn2_done")
        ln2_stats = sem("ln2_stats")
        bn3_done = sem("bn3_done")
        ln3_stats = sem("ln3_stats")
        ln_pool = sem("ln_pool")
        ln_scale = sem("ln_scale")
        nh_ready = sem("nh_ready")
        nhg_ready = sem("nhg_ready")
        xb_ready = sem("xb_ready")
        x1_ready = sem("x1_ready")
        n3_ready = sem("n3_ready")
        n3T_mm = sem("n3T_mm")
        h3T_ready = sem("h3T_ready")
        up_mm = sem("up_mm")
        gelu_done = sem("gelu_done")
        down_mm = sem("down_mm")
        yT_ready = sem("yT_ready")
        y_mm = sem("y_mm")
        out_ready = sem("out_ready")

        def tiles(buf, g, w=D):
            return buf[:, bass.ds(g * TILES, TILES), 0:w]

        def used(eng, s, value):
            if not isinstance(value, int) or value > 0:
                eng.wait_ge(s, value)

        def apart(eng):
            eng.nop(nofuse=True)

        def bc(ap, shape):
            return ap.to_broadcast(shape)

        def per_tile(rep, b):
            return bc(rep[:, bass.ds(b, 1), :], [P, TILES, D])

        def stage(t):
            return 16 * (2 ** t - 1), 4 * 2 ** t

        def run(eng, first, last, step):
            for n in first:
                step(n // 2, n % 2)
            with eng.Fori(last[0], last[1]) as b:
                step(b, 0)
                step(b, 1)

        block = ctx.enter_context(nc.Block())

        @block.sync
        def _(sp):
            sp.dma_start(x[:, 0:4, :], x_v[:, 0, 0:4, :]).then_inc(x_ld[0], 16)
            sp.wait_ge(rows_clear, 1)
            sp.dma_start(rows[0:4, :], c_in).then_inc(rows_in, 16)
            sp.dma_start(rows[4:8, :], up_bias.rearrange("(a d) -> a d", d=P)).then_inc(rows_in, 16)
            sp.dma_start(rows[8:12, :], b_exp.rearrange("(a d) -> a d", d=P)).then_inc(rows_in, 16)
            for i, v in enumerate((b_con, down_bias, bd)):
                sp.dma_start(rows[12 + i:13 + i, :], v.rearrange("(a d) -> a d", a=1)).then_inc(rows_in, 16)
            for g in range(1, GROUPS):
                h = g % 2 * 4
                sp.dma_start(x[:, 4 * g:4 * g + 4, :], x_v[:, g // 2, h:h + 4, :]).then_inc(x_ld[g], 16)
            for i, w in enumerate((up_w, down_w)):
                sp.dma_start(raw_big[i][:, :], bass.AP(tensor=w.tensor, offset=w.offset + SMALL * HID * 2,
                                                       ap=[[0, P], [1, 2048]])).then_inc(big_in[i], 16)
            sp.dma_start(wexp_s[:, :], W_exp).then_inc(ffn_in, 16)
            sp.dma_start(wcon_s[:, :, :], W_con.rearrange("(c p) d -> p c d", p=P)).then_inc(ffn_in, 16)

            def store(b, k):
                g = 2 * b + k
                sp.wait_ge(out_ready, g + 1)
                sp.dma_start(out_v[:, bass.ds(b, 1), 4 * k:4 * k + 4, :].squeeze(1),
                             tiles(x, g)).then_inc(stored, 16)

            with sp.Fori(0, B) as b:
                store(b, 0)
                store(b, 1)
            sp.wait_ge(stored, 16 * GROUPS)

        @block.gpsimd
        def _(pool):
            pool.memset(rows[:, :], 0.0).then_inc(rows_clear, 1)
            pool.memset(ident[:, :], 0.0).then_inc(id_zero, 1)
            pool.wait_ge(id_zero, 1)
            pool.affine_select(out=ident[:, :], in_=ident[:, :], compare_op=ALU.not_equal, fill=1.0, base=0,
                               pattern=[[-1, P]], channel_multiplier=1).then_inc(id_ready, 1)
            pool.memset(power[:, :], -0.5).then_inc(power_ready, 1)
            pool.memset(eps1[:, :], LN_EPS).then_inc(power_ready, 1)
            pool.memset(eps23[:, 0:4], ATTN_LN_EPS).then_inc(power_ready, 1)
            pool.memset(eps23[:, 4:8], LN_EPS).then_inc(power_ready, 1)
            pool.memset(ones[:, :], 1.0).then_inc(const_ready, 1)
            pool.memset(ones_bf[:, :], 1.0).then_inc(const_ready, 1)
            pool.memset(bias3[:, :], 0.0).then_inc(const_ready, 1)
            pool.memset(r[:, :, D:D + 1], 1.0).then_inc(const_ready, 1)

            def ln1(b, tile0, n, stats):
                m0 = tile0 if n == 4 else 0
                pool.wait_ge(ln1_stats, stats)
                pool.tensor_tensor(ve1[:, 0:n], mv1[:, m0:m0 + n, 1], eps1[:, 0:n], ALU.add).then_inc(ln1_pool, 1)
                pool.tensor_scalar(nm1[:, 0:n], mv1[:, m0:m0 + n, 0], -1.0, None, ALU.mult).then_inc(ln1_pool, 1)
                pool.wait_ge(ln1_pool, 3 * b + 2)
                apart(pool)
                pool.tensor_tensor(rs1[:, bass.ds(tile0, n)], ve1[:, 0:n], power[:, 0:n], ALU.pow).then_inc(ln1_pool, 1)
                pool.wait_ge(ln1_pool, 3 * b + 3)
                apart(pool)
                pool.tensor_tensor(nb1[:, bass.ds(tile0, n)], nm1[:, 0:n], rs1[:, bass.ds(tile0, n)],
                                   ALU.mult).then_inc(ln1_scale, 1)

            pool.wait_ge(power_ready, 4)
            ln1(0, 0, 4, 1)

            pool.memset(sel[:, :, :, :], 0.0).then_inc(sel_zero, 1)
            pool.wait_ge(sel_zero, 1)
            for t in range(SMALL):
                for i in range(2):
                    v = sel[0:64 >> t, t, i, :].rearrange("h (a b l) -> h a b l", b=2, l=2 ** t)[:, :, i, :]
                    pool.affine_select(out=v, in_=v, compare_op=ALU.not_equal, fill=1.0, base=0,
                                       pattern=[[-1, 64 >> t], [0, 2 ** t]],
                                       channel_multiplier=1).then_inc(sel_ready, 1)
            ln1(1, 4, 4, 2)
            pool.memset(head_mask[:, :], 1.0).then_inc(mask_step, 1)
            hm = head_mask[:, :].rearrange("p (h e) -> p h e", e=HD)
            pool.wait_ge(mask_step, 1)
            pool.affine_select(out=hm, in_=hm, compare_op=ALU.is_ge, fill=0.0, base=0,
                               pattern=[[-HD, HEADS], [0, HD]], channel_multiplier=1).then_inc(mask_step, 1)
            pool.wait_ge(mask_step, 2)
            pool.affine_select(out=hm, in_=hm, compare_op=ALU.is_ge, fill=0.0, base=HD - 1,
                               pattern=[[HD, HEADS], [0, HD]], channel_multiplier=-1).then_inc(mask_step, 1)

            pool.wait_ge(rep_copied, 2 * B)

            def step_a(b, k):
                g = 2 * b + k
                if k == 0 and not (isinstance(b, int) and b == B - 1):
                    ln1(b + 2, 8 * b + 8, 8, 2 * b + 4)
                pool.wait_ge(n1_ready, g + 1)
                apart(pool)
                pool.tensor_tensor(tiles(r, g), n1[:, k, :, :], per_tile(scale_rep, b), ALU.mult).then_inc(r_half, 1)
                pool.wait_ge(r_half, g + 1)
                apart(pool)
                pool.tensor_tensor(tiles(r, g), tiles(r, g), per_tile(shift_rep, b), ALU.add).then_inc(r_ready, 1)

            step_a(0, 0)
            step_a(0, 1)
            with pool.Fori(1, B - 1) as b:
                step_a(b, 0)
                step_a(b, 1)
            step_a(B - 1, 0)
            step_a(B - 1, 1)

            pool.wait_ge(gate_ready, 1)
            pool.wait_ge(reps_in, 48)
            for b in range(B):
                pool.tensor_tensor(gg_rep[:, b, :], ga_rep[:, b, :], gamma_rep[:, :], ALU.mult).then_inc(gate_step, 1)
                pool.tensor_tensor(gbeta_rep[:, b, :], ga_rep[:, b, :], beta_rep[:, :], ALU.mult).then_inc(gate_step, 1)
            pool.wait_ge(gate_step, 3 + 2 * B)

            def divisor(b, k):
                g = 2 * b + k
                used(pool, den_ready, g)
                apart(pool)
                pool.tensor_tensor(qk[:, :, :], tiles(q, g), per_tile(ks_rep, b), ALU.mult).then_inc(qks_ready, 1)

            def step_b(b, k, attn=True, prev=True, more=True):
                g = 2 * b + k
                if prev:
                    bp = b - 1 + k
                    pool.wait_ge(nh_ready, g)
                    apart(pool)
                    pool.tensor_tensor(nh[:, 1 - k, :, :], nh[:, 1 - k, :, :], per_tile(gg_rep, bp),
                                       ALU.mult).then_inc(nhg_ready, 1)
                if more:
                    if k == 0:
                        divisor(b, 1)
                    else:
                        divisor(b + 1, 0)
                if attn:
                    pool.tensor_tensor(tiles(x, g), tiles(x, g), per_tile(gbeta_rep, b), ALU.add).then_inc(xb_ready, 1)
                lo, hi = (0 if attn else 4), (8 if prev else 4)
                if attn:
                    pool.wait_ge(ln2_stats, g + 1)
                if prev:
                    pool.wait_ge(ln3_stats, g)
                    used(pool, n3_ready, g - 2)
                used(pool, nh_ready, g - 1)
                pool.tensor_tensor(ve[:, lo:hi], mv[:, k, lo:hi, 1], eps23[:, lo:hi], ALU.add).then_inc(ln_pool, 1)
                pool.tensor_scalar(nm[:, lo:hi], mv[:, k, lo:hi, 0], -1.0, None, ALU.mult).then_inc(ln_pool, 1)
                pool.wait_ge(ln_pool, 3 * g + 2)
                pool.tensor_tensor(rs[:, k, lo:hi], ve[:, lo:hi], power[:, lo:hi], ALU.pow).then_inc(ln_pool, 1)
                pool.wait_ge(ln_pool, 3 * g + 3)
                pool.tensor_tensor(nb[:, k, lo:hi], nm[:, lo:hi], rs[:, k, lo:hi], ALU.mult).then_inc(ln_scale, 1)

            pool.wait_ge(ksrep_saved, 1)
            divisor(0, 0)
            step_b(0, 0, prev=False)
            step_b(0, 1)
            with pool.Fori(1, B - 1) as b:
                step_b(b, 0)
                step_b(b, 1)
            step_b(B - 1, 0)
            step_b(B - 1, 1, more=False)
            step_b(B, 0, attn=False, more=False)

        @block.scalar
        def _(sc_e):
            for i, w in enumerate((Wq, Wk, Wv, Wd)):
                sc_e.dma_start(w_raw[:, i, :], w).then_inc(w_in, 16)
            sc_e.dma_start(wmod_s[:, :], wmod).then_inc(wmod_in, 16)
            for i, v in enumerate((bq, bk)):
                sc_e.dma_start(bias_in[:, i * D:(i + 1) * D],
                               bass.AP(tensor=v.tensor, offset=v.offset, ap=[[0, 3], [1, D]])).then_inc(bias_ld, 16)
            for dst, v in ((bd_rep, bd), (gamma_rep, gamma), (beta_rep, beta)):
                sc_e.dma_start(dst[:, :], bass.AP(tensor=v.tensor, offset=v.offset,
                                                  ap=[[0, P], [1, D]])).then_inc(reps_in, 16)
            sc_e.dma_start(bv_row[:, :], bv.rearrange("(a d) -> a d", a=1)).then_inc(bv_in, 16)
            for i, w in enumerate((up_w, down_w)):
                for t in range(SMALL):
                    at, n = stage(t)
                    src = bass.AP(tensor=w.tensor, offset=w.offset + t * HID * 2, ap=[[n, 64 >> t], [256, CH], [1, n]])
                    dst = raw_small[i][0:64 >> t, at:at + CH * n].rearrange("h (c n) -> h c n", c=CH)
                    sc_e.dma_start(dst, src).then_inc(small_in[i], 16)

            sc_e.wait_ge(cols_copied, 1)
            sc_e.activation(sig[:, 0, :], cols[:, 0:4], ACT.Exp, scale=-1.0).then_inc(silu_exp, 1)
            sc_e.wait_ge(wT_ready, 1)
            sc_e.copy(wT[:, :, :], bank[1][:, :].rearrange("p (a b) -> p a b", a=4)).then_inc(wT_copied, 1)

            def norm1(b, k):
                g = 2 * b + k
                used(sc_e, n1T_ready, g - 1)
                used(sc_e, r_ready, g - 1)
                apart(sc_e)
                for t in range(TILES):
                    s = g * TILES + t
                    ins = sc_e.activation(n1[:, k, t, :], x[:, bass.ds(s, 1), :].squeeze(1), ACT.Identity,
                                          bias=nb1[:, bass.ds(s, 1)], scale=rs1[:, bass.ds(s, 1)])
                ins.then_inc(n1_ready, 1)

            def shift_scale(b, k):
                g = 2 * b + k
                sc_e.wait_ge(n1T_ready, g + 1)
                used(sc_e, qk_ready, 2 * (g - 1))
                apart(sc_e)
                sc_e.activation(hT[:, k, :], bank[k][:, :], ACT.Identity, bias=modc[:, 0, bass.ds(b, 1)],
                                scale=modc[:, 1, bass.ds(b, 1)]).then_inc(hT_ready, 1)

            def exps(b, k):
                g = 2 * b + k
                for h in range(2):
                    sc_e.wait_ge(qk_ready, 2 * g + h + 1)
                    used(sc_e, phi_ready, 2 * (g - 1) + h + 1)
                    sc_e.activation(ev[:, h, :], bank[2 + 2 * k + h][:, :], ACT.Relu, bias=1.0,
                                    scale=-1.0).then_inc(relu_ready, 1)
                for h in range(2):
                    sc_e.wait_ge(relu_ready, 2 * g + h + 1)
                    sc_e.activation(e[:, h, :], ev[:, h, :], ACT.Exp, scale=-1.0).then_inc(exp_ready, 1)

            sc_e.wait_ge(ln1_scale, 1)
            norm1(0, 0)
            for b in range(B):
                sc_e.wait_ge(mod_rep, b + 1)
                sc_e.copy(ga_rep[:, b, :], bank[2 + b][:, 2 * D:3 * D]).then_inc(ga_copied, 1)
            sc_e.wait_ge(modc_ready, 1)
            shift_scale(0, 0)
            sc_e.wait_ge(ln1_scale, 2)
            norm1(0, 1)
            shift_scale(0, 1)
            exps(0, 0)
            sc_e.wait_ge(ln1_scale, 3)
            norm1(1, 0)
            with sc_e.Fori(1, B - 1) as b:
                shift_scale(b, 0)
                exps(b - 1, 1)
                norm1(b, 1)
                shift_scale(b, 1)
                exps(b, 0)
                sc_e.wait_ge(ln1_scale, b + 3)
                norm1(b + 1, 0)
            shift_scale(B - 1, 0)
            exps(B - 2, 1)
            norm1(B - 1, 1)
            shift_scale(B - 1, 1)
            exps(B - 1, 0)
            exps(B - 1, 1)

            sc_e.wait_ge(gT_mm, 1)
            sc_e.copy(gT[:, :, :], bank[0][:, :].rearrange("p (a b) -> p a b", a=B)).then_inc(gT_saved, 1)
            sc_e.wait_ge(ksrep_mm, 1)
            sc_e.copy(ks_rep[:, :, :], bank[2][:, :].rearrange("p (a b) -> p a b", a=B)).then_inc(ksrep_saved, 1)
            sc_e.wait_ge(m_mm, 1)
            sc_e.copy(m_mat[:, :, :], bank[4][:, :].rearrange("p (a b) -> p a b", a=B)).then_inc(m_saved, 1)

            def attn_T(b, k):
                g = 2 * b + k
                sc_e.wait_ge(qnT_mm, g + 1)
                used(sc_e, attn_mm, g - 1)
                sc_e.copy(qT[:, k, :], bank[0][:, :]).then_inc(qT_ready, 1)

            def norm2(b, k):
                g = 2 * b + k
                sc_e.wait_ge(ln_scale, g + 1)
                used(sc_e, x1_ready, g - 1)
                for t in range(TILES):
                    ins = sc_e.activation(nh[:, k, t, :], hs[:, k, t, :], ACT.Identity,
                                          bias=nb[:, k, t:t + 1], scale=rs[:, k, t:t + 1])
                ins.then_inc(nh_ready, 1)

            def ffn_in_T(b, k):
                g = 2 * b + k
                sc_e.wait_ge(n3T_mm, g + 1)
                used(sc_e, up_mm, CH * (g - 1))
                apart(sc_e)
                sc_e.activation(h3T[:, k, :], bank[2][:, :], ACT.Identity, bias=modc[:, 3, bass.ds(b, 1)],
                                scale=modc[:, 4, bass.ds(b, 1)]).then_inc(h3T_ready, 1)

            def gelu(b, k, c):
                g = 2 * b + k
                sc_e.wait_ge(up_mm, CH * g + c + 1)
                if c == 0:
                    used(sc_e, down_mm, g - 1)
                sc_e.activation(act[:, k, c, :], bank[3 + c % 3][:, :], ACT.Gelu,
                                bias=b_up[:, c:c + 1]).then_inc(gelu_done, 1)

            def gate_y(b, k):
                g = 2 * b + k
                sc_e.wait_ge(down_mm, g + 1)
                used(sc_e, y_mm, g - 1)
                apart(sc_e)
                sc_e.activation(yT[:, k, :], bank[6][:, :], ACT.Identity, bias=gbc[:, 1, bass.ds(b, 1)],
                                scale=gbc[:, 0, bass.ds(b, 1)]).then_inc(yT_ready, 1)

            def step_b(b, k, attn=True, ffn=True, last=True):
                if ffn:
                    ffn_in_T(b - 1, k)
                if attn:
                    attn_T(b, k)
                if last:
                    gate_y(b - 2 + k, 1 - k)
                if ffn:
                    for c in range(CH - 1):
                        gelu(b - 1, k, c)
                if attn:
                    norm2(b, k)
                if ffn:
                    gelu(b - 1, k, CH - 1)

            step_b(0, 0, ffn=False, last=False)
            sc_e.wait_ge(wexpT_mm, 1)
            sc_e.copy(wexpT[:, :, :], bank[3][:, :].rearrange("p (a b) -> p a b", a=CH)).then_inc(wexpT_saved, 1)
            sc_e.wait_ge(wup_mm, 1)
            sc_e.copy(w_up[:, :], bank[4][:, :]).then_inc(wup_saved, 1)
            attn_T(0, 1)
            for ic in range(CH):
                sc_e.wait_ge(td_mm, ic + 1)
                sc_e.copy(t_down[:, ic, :], bank[6 + ic % 2][:, :]).then_inc(td_saved, 1)
            sc_e.wait_ge(wdown_mm, 1)
            sc_e.copy(w_down[:, :, :], bank[3][:, :].rearrange("p (a b) -> p a b", a=CH)).then_inc(wdown_saved, 1)
            norm2(0, 1)
            sc_e.preload_act_table(ACT.Gelu)
            sc_e.wait_ge(bup_saved, 1)
            step_b(1, 0, last=False)
            step_b(1, 1)
            with sc_e.Fori(2, B) as b:
                step_b(b, 0)
                step_b(b, 1)
            step_b(B, 0, attn=False)
            step_b(B, 1, attn=False)
            gate_y(B - 1, 1)

        @block.vector
        def _(dve):
            def stats1(b, k):
                g = 2 * b + k
                used(dve, ln1_stats, g - 1)
                for t in range(TILES):
                    ins = dve.bn_stats(bn1[:, k, t, :], x[:, bass.ds(g * TILES + t, 1), :].squeeze(1))
                ins.then_inc(bn1_done, 1)
                dve.wait_ge(bn1_done, g + 1)
                if not isinstance(b, int) or b > 0:
                    dve.wait_ge(ln1_pool, 3 * b + 2)
                apart(dve)
                for t in range(TILES):
                    ins = dve.bn_aggr(mv1[:, k * TILES + t, :], bn1[:, k, t, :])
                ins.then_inc(ln1_stats, 1)

            dve.wait_ge(x_ld[0], 16)
            stats1(0, 0)
            dve.wait_ge(cols_ready, 1)
            dve.tensor_copy(cols[:, :], bank[0][:, 0:15]).then_inc(cols_copied, 1)
            dve.wait_ge(silu_exp, 1)
            dve.tensor_scalar(sig[:, 1, :], sig[:, 0, :], 1.0, None, ALU.add).then_inc(silu_step, 1)
            dve.wait_ge(silu_step, 1)
            dve.reciprocal(sig[:, 2, :], sig[:, 1, :]).then_inc(silu_step, 1)
            dve.wait_ge(silu_step, 2)
            dve.tensor_tensor(sc[:, :], cols[:, 0:4], sig[:, 2, :], ALU.mult).then_inc(sc_ready, 1)
            dve.wait_ge(sc_ready, 1)
            dve.tensor_copy(sc_rep[:, :, :], bc(sc[:, :].unsqueeze(2), [P, B, P])).then_inc(sc_rep_ready, 1)
            dve.wait_ge(x_ld[1], 16)
            stats1(0, 1)
            dve.wait_ge(modT_ready, 1)
            dve.tensor_copy(modc[:, :, :], bank[0][:, 16:40].rearrange("p (j b) -> p j b", j=6)).then_inc(modc_step, 1)
            dve.wait_ge(modc_step, 1)
            for j in (1, 4):
                dve.tensor_scalar(modc[:, j, :], modc[:, j, :], 1.0, None, ALU.add).then_inc(modc_step, 1)
            dve.tensor_tensor(bsum[:, :], cols[:, 12:13], cols[:, 13:14], ALU.add).then_inc(modc_step, 1)
            dve.tensor_scalar(gbw[:, 0, :], modc[:, 5, :], 0.0, 2.0, ALU.is_ge, ALU.mult).then_inc(modc_step, 1)
            dve.scalar_tensor_tensor(out=gbw[:, 1, :], in0=modc[:, 5, :], scalar=-1.0, in1=modc[:, 5, :],
                                     op0=ALU.mult, op1=ALU.max).then_inc(modc_step, 1)
            dve.wait_ge(modc_step, 6)
            dve.tensor_scalar(gbw[:, 2, :], gbw[:, 1, :], GATE_FLOOR, None, ALU.max).then_inc(modc_step, 1)
            dve.wait_ge(modc_step, 7)
            dve.scalar_tensor_tensor(out=gbc[:, 0, :], in0=gbw[:, 0, :], scalar=-1.0, in1=gbw[:, 2, :],
                                     op0=ALU.add, op1=ALU.mult).then_inc(modc_step, 1)
            dve.wait_ge(modc_step, 8)
            dve.tensor_scalar(gbc[:, 1, :], gbc[:, 0, :], bsum[:, 0:1], None, ALU.mult).then_inc(modc_ready, 1)

            dve.wait_ge(bias_ld, 32)
            dve.wait_ge(id_ready, 1)
            dve.tensor_scalar(bias_in[:, :], bias_in[:, :], 1.0, None, ALU.add).then_inc(bias_step, 1)
            dve.wait_ge(bias_step, 1)
            dve.tensor_copy(bias_b[:, :], bias_in[:, :]).then_inc(bias_step, 1)
            dve.wait_ge(bias_step, 2)
            dve.tensor_tensor(bias_r[:, :], bias_in[:, :], bias_b[:, :], ALU.subtract).then_inc(bias_step, 1)
            dve.wait_ge(bias_step, 3)
            dve.tensor_copy(bias_b2[:, :], bias_r[:, :]).then_inc(bias_step, 1)
            dve.tensor_scalar(bias_m[:, :], bias_b[:, :], ident[0:3, 0:1], None, ALU.mult).then_inc(bias_step, 1)
            dve.wait_ge(bias_step, 5)
            dve.tensor_tensor(bias_r2[:, :], bias_r[:, :], bias_b2[:, :], ALU.subtract).then_inc(bias_step, 1)
            dve.scalar_tensor_tensor(out=bias_m2[:, :], in0=bias_b2[:, :], scalar=ident[0:3, 1:2], in1=bias_m[:, :],
                                     op0=ALU.mult, op1=ALU.add).then_inc(bias_step, 1)
            dve.wait_ge(bias_step, 7)
            dve.wait_ge(const_ready, 4)
            dve.scalar_tensor_tensor(out=bias3[0:3, :], in0=bias_r2[:, :], scalar=ident[0:3, 2:3], in1=bias_m2[:, :],
                                     op0=ALU.mult, op1=ALU.add).then_inc(bias_ready, 1)
            dve.wait_ge(reps_in, 48)
            for b in range(B):
                dve.wait_ge(ga_copied, b + 1)
                dve.tensor_scalar(scale_rep[:, b, :], bank[2 + b][:, D:2 * D], 1.0, None, ALU.add).then_inc(rep_copied, 1)
                dve.tensor_tensor(shift_rep[:, b, :], bank[2 + b][:, 0:D], bd_rep[:, :], ALU.add).then_inc(rep_copied, 1)
            dve.wait_ge(vb_mm, 1)
            dve.wait_ge(bv_in, 16)
            dve.tensor_tensor(vb_row[:, :], bv_row[:, :], bank[0][0:1, 128:256], ALU.subtract).then_inc(vb_ready, 1)

            def product(i, t):
                n = 2 ** (t + 1)
                at, before = 4 * (n - 2), 4 * (n // 2 - 2)
                steps = prod_step[i]
                if t == 0:
                    dve.tensor_copy(prod[i][:, 0:8], bank[6][:, 0:8]).then_inc(steps, 1)
                    return
                dve.wait_ge(steps, t)
                if t < NS - 1:
                    o = prod[i][:, at:at + CH * n].rearrange("p (c o l) -> p c o l", c=CH, o=2)
                else:
                    o = t_mat[i][:, :, :].rearrange("p c (o l) -> p c o l", o=2)
                prev = prod[i][:, before:before + CH * n // 2].rearrange("p (c l) -> p c l", c=CH)
                if t < SMALL:
                    f = (bank[6][:, at:at + CH * n] if t < 6 else bank[7][:, :]).rearrange("p (c o l) -> p c o l", c=CH, o=2)
                    dve.tensor_tensor(o, bc(prev.unsqueeze(2), [P, CH, 2, n // 2]), f, ALU.mult).then_inc(steps, 1)
                elif t == SMALL:
                    f = raw_big[i][:, 0:1024].rearrange("p (k l o i) -> p k i o l", k=2, o=2, i=2)
                    for k in range(2):
                        ins = dve.tensor_tensor(o[:, 2 * k:2 * k + 2],
                                                bc(prev[:, 2 * k:2 * k + 2, :].unsqueeze(2), [P, 2, 2, n // 2]),
                                                f[:, k], ALU.mult)
                    ins.then_inc(steps, 1)
                else:
                    f = raw_big[i][:, 1024:2048].rearrange("p (l o i) -> p i o l", o=2, i=2)
                    for c in range(CH):
                        ins = dve.tensor_tensor(o[:, c], bc(prev[:, c, :].unsqueeze(1), [P, 2, n // 2]),
                                                f[:, c // 2], ALU.mult)
                    ins.then_inc(steps, 1)

            dve.wait_ge(x_ld[2], 16)
            stats1(1, 0)
            dve.wait_ge(factors_ready, 1)
            for t in range(SMALL):
                product(0, t)

            def phi(b, k):
                g = 2 * b + k
                used(dve, g_done, g - 1)
                for h in range(2):
                    dve.wait_ge(exp_ready, 2 * g + h + 1)
                    em = e[:, h, :].rearrange("p (t w d) -> p t w d", t=2, w=2)
                    pv = bank[2 + 2 * k + h][:, :].rearrange("p (t w d) -> p t w d", t=2, w=2)
                    dve.tensor_tensor(kf[:, k, 2 * h:2 * h + 2, :], em[:, :, 1, :], pv[:, :, 1, :], ALU.max)
                    dve.tensor_tensor(q[:, bass.ds(TILES * g + 2 * h, 2), :], em[:, :, 0, :], pv[:, :, 0, :],
                                      ALU.max).then_inc(phi_ready, 1)

            def save_g(b):
                dve.wait_ge(g_done, 2 * b + 2)
                dve.tensor_copy(gs[:, bass.ds(b, 1), :].squeeze(1), bank[6][:, 0:D + 1]).then_inc(g_saved, 1)

            dve.wait_ge(x_ld[3], 16)
            stats1(1, 1)
            phi(0, 0)
            dve.wait_ge(factors_ready, 2)
            for t in range(SMALL):
                product(1, t)
            for g in range(4, GROUPS):
                dve.wait_ge(x_ld[g], 16)
            with dve.Fori(1, B - 1) as b:
                stats1(b + 1, 0)
                phi(b - 1, 1)
                stats1(b + 1, 1)
                phi(b, 0)
                save_g(b - 1)
            phi(B - 2, 1)
            phi(B - 1, 0)
            save_g(B - 2)
            phi(B - 1, 1)
            save_g(B - 1)

            dve.wait_ge(g_saved, B)
            dve.tensor_scalar(ks_eps[:, :], gs[:, :, D], ATTN_EPS, None, ALU.add).then_inc(ks_eps_ready, 1)
            dve.wait_ge(ks_eps_ready, 1)
            for b in range(B):
                ins = dve.tensor_scalar(ks_diag[:, b, :], ident[:, :], ks_eps[:, b:b + 1], None, ALU.mult)
            ins.then_inc(ks_diag_ready, 1)
            dve.wait_ge(ks_mm, 1)
            dve.tensor_copy(ks_row[:, :, :], bank[1][0:1, :].rearrange("p (a b) -> p a b", a=B)).then_inc(ks_saved, 1)
            dve.wait_ge(kv_mm, 1)
            dve.wait_ge(mask_step, 3)
            dve.tensor_tensor(kvT[:, :, :], bank[3][:, :].rearrange("p (a b) -> p a b", a=B),
                              bc(head_mask[:, :].unsqueeze(1), [P, B, P]), ALU.mult).then_inc(kv_saved, 1)

            def divide(b, k):
                g = 2 * b + k
                dve.wait_ge(qks_ready, g + 1)
                used(dve, z_ready, g)
                dve.reduce_sum(den[:, :], qk[:, :, :].rearrange("p t (h e) -> p (t h) e", e=HD), AX_X).then_inc(den_ready, 1)
                dve.wait_ge(den_ready, g + 1)
                used(dve, qn_ready, g)
                dve.reciprocal(z[:, :], den[:, :]).then_inc(z_ready, 1)
                dve.wait_ge(z_ready, g + 1)
                used(dve, qnT_mm, g - 1)
                dve.tensor_tensor(qn[:, k, :, :].rearrange("p t (h e) -> p (t h) e", e=HD),
                                  tiles(q, g).rearrange("p t (h e) -> p (t h) e", e=HD),
                                  bc(z[:, :].unsqueeze(2), [P, TILES * HEADS, HD]), ALU.mult).then_inc(qn_ready, 1)

            def step_b(b, k, attn=True, prev=True, more=True, norm=True, final=True):
                g = 2 * b + k
                if prev:
                    dve.wait_ge(nhg_ready, g)
                    dve.wait_ge(xb_ready, g)
                    dve.tensor_tensor(tiles(x, g - 1), nh[:, 1 - k, :, :], tiles(x, g - 1), ALU.add).then_inc(x1_ready, 1)
                    dve.wait_ge(x1_ready, g)
                    used(dve, ln3_stats, g - 1)
                    for t in range(TILES):
                        ins = dve.bn_stats(bn3[:, t, :], x[:, bass.ds(TILES * (g - 1) + t, 1), :].squeeze(1))
                    ins.then_inc(bn3_done, 1)
                    dve.wait_ge(bn3_done, g)
                    for t in range(TILES):
                        ins = dve.bn_aggr(mv[:, k, 4 + t, :], bn3[:, t, :])
                    ins.then_inc(ln3_stats, 1)
                if attn:
                    dve.wait_ge(attn_mm, g + 1)
                    dve.wait_ge(r_ready, g + 1)
                    used(dve, nh_ready, g - 1)
                    dve.tensor_tensor(hs[:, k, :, :], bank[1][:, :].rearrange("p (t d) -> p t d", t=TILES),
                                      tiles(r, g), ALU.add).then_inc(hs_ready, 1)
                    dve.wait_ge(hs_ready, g + 1)
                    used(dve, ln2_stats, g)
                    for t in range(TILES):
                        ins = dve.bn_stats(bn2[:, t, :], hs[:, k, t, :])
                    ins.then_inc(bn2_done, 1)
                    dve.wait_ge(bn2_done, g + 1)
                    for t in range(TILES):
                        ins = dve.bn_aggr(mv[:, k, t, :], bn2[:, t, :])
                    ins.then_inc(ln2_stats, 1)
                if more:
                    if k == 0:
                        divide(b, 1)
                    else:
                        divide(b + 1, 0)
                if final:
                    dve.wait_ge(y_mm, g - 2)
                    dve.tensor_tensor(tiles(x, g - 3), bank[7][:, :].rearrange("p (t d) -> p t d", t=TILES),
                                      tiles(x, g - 3), ALU.add).then_inc(out_ready, 1)
                if norm:
                    dve.wait_ge(ln_scale, g + 1)
                    used(dve, n3T_mm, g - 2)
                    for t in range(TILES):
                        ins = dve.tensor_scalar(n3[:, 1 - k, t, :], x[:, bass.ds(TILES * (g - 1) + t, 1), :].squeeze(1),
                                                rs[:, k, 4 + t:5 + t], nb[:, k, 4 + t:5 + t], ALU.mult, ALU.add)
                    ins.then_inc(n3_ready, 1)

            dve.wait_ge(ga_copied, B)
            dve.tensor_scalar(ga_sign[:, :, :], ga_rep[:, :, :], 0.0, 2.0, ALU.is_ge, ALU.mult).then_inc(gate_step, 1)
            dve.scalar_tensor_tensor(out=ga_abs[:, :, :], in0=ga_rep[:, :, :], scalar=-1.0, in1=ga_rep[:, :, :],
                                     op0=ALU.mult, op1=ALU.max).then_inc(gate_step, 1)
            dve.wait_ge(gate_step, 2)
            dve.tensor_scalar(ga_abs[:, :, :], ga_abs[:, :, :], GATE_FLOOR, None, ALU.max).then_inc(gate_step, 1)
            dve.wait_ge(gate_step, 3)
            dve.scalar_tensor_tensor(out=ga_rep[:, :, :], in0=ga_sign[:, :, :], scalar=-1.0, in1=ga_abs[:, :, :],
                                     op0=ALU.add, op1=ALU.mult).then_inc(gate_ready, 1)
            divide(0, 0)
            dve.wait_ge(big_in[0], 16)
            product(0, 7)
            product(0, 8)
            step_b(0, 0, prev=False, norm=False, final=False)
            dve.wait_ge(big_in[1], 16)
            product(1, 7)
            product(1, 8)
            step_b(0, 1, final=False)
            dve.wait_ge(bup_mm, 1)
            dve.tensor_tensor(b_up[:, :], bank[5][:, 0:CH], cols[:, 4:8], ALU.add).then_inc(bup_saved, 1)
            step_b(1, 0, final=False)
            step_b(1, 1)
            with dve.Fori(2, B - 1) as b:
                step_b(b, 0)
                step_b(b, 1)
            step_b(B - 1, 0)
            step_b(B - 1, 1, more=False)
            step_b(B, 0, attn=False, more=False)
            step_b(B, 1, attn=False, prev=False, more=False, norm=False)
            step_b(B + 1, 0, attn=False, prev=False, more=False, norm=False)

        @block.tensor
        def _(pe):
            pe.wait_ge(id_ready, 1)
            pe.wait_ge(rows_in, 96)
            pe.transpose(bank[0][:, 0:15], rows[0:15, :], ident[0:15, 0:15]).then_inc(cols_ready, 1)
            pe.wait_ge(w_in, 64)
            for i in range(4):
                ins = pe.transpose(bank[1][:, i * P:(i + 1) * P], w_raw[:, i, :], ident[:, :])
            ins.then_inc(wT_ready, 1)
            pe.wait_ge(wmod_in, 16)
            pe.wait_ge(sc_ready, 1)
            pe.wait_ge(cols_copied, 1)
            for j in range(6):
                ins = pe.matmul(bank[0][:, 16 + 4 * j:20 + 4 * j], wmod_s[:, j * D:(j + 1) * D], sc[:, :],
                                start=True, stop=True)
            ins.then_inc(modT_ready, 1)
            pe.wait_ge(sc_rep_ready, 1)
            for b in range(B):
                pe.matmul(bank[2 + b][:, 0:3 * D], sc_rep[:, b, :], wmod_s[:, 0:3 * D],
                          start=True, stop=True).then_inc(mod_rep, 1)
            pe.wait_ge(wT_copied, 1)
            pe.wait_ge(modc_step, 1)
            pe.matmul(bank[0][0:1, 128:256], cols[:, 14:15], wT[:, 2, :], start=True, stop=True).then_inc(vb_mm, 1)

            def factors(i):
                pe.wait_ge(small_in[i], 16 * SMALL)
                for t in range(SMALL):
                    at, n = stage(t)
                    w = raw_small[i][0:64 >> t, at:at + CH * n].rearrange("h (c l o i) -> h i c o l", c=CH, o=2, i=2)
                    o = bank[6][:, 4 * (2 ** (t + 1) - 2):][:, 0:CH * 2 ** (t + 1)] if t < 6 else bank[7][:, :]
                    for j in range(2):
                        ins = pe.matmul(o, sel[0:64 >> t, t, j, :], w[:, j], start=(j == 0), stop=(j == 1))
                ins.then_inc(factors_ready, 1)

            pe.wait_ge(sel_ready, 2 * SMALL)
            factors(0)

            def transposes1(b, k):
                g = 2 * b + k
                pe.wait_ge(n1_ready, g + 1)
                used(pe, hT_ready, g - 1)
                for t in range(TILES):
                    ins = pe.transpose(bank[k][:, t * P:(t + 1) * P], n1[:, k, t, :], ident[:, :])
                ins.then_inc(n1T_ready, 1)

            def qk_product(b, k):
                g = 2 * b + k
                pe.wait_ge(hT_ready, g + 1)
                for t in range(TILES):
                    if t % 2 == 0:
                        used(pe, phi_ready, 2 * (g - 2) + t // 2 + 1)
                    o = bank[2 + 2 * k + t // 2][:, t % 2 * 256:t % 2 * 256 + 256]
                    pe.matmul(o, ones_bf[:, :], bias3[:, :], start=True, stop=False)
                    ins = pe.matmul(o, hT[:, k, t * P:(t + 1) * P], wT[:, 0:2, :], start=False, stop=True)
                    if t % 2:
                        ins.then_inc(qk_ready, 1)

            def sums(b, k):
                g = 2 * b + k
                pe.wait_ge(phi_ready, 2 * g + 2)
                pe.wait_ge(r_ready, g + 1)
                if k == 0:
                    used(pe, g_saved, b)
                for t in range(TILES):
                    ins = pe.matmul(bank[6][:, 0:D + 1], kf[:, k, t, :], r[:, bass.ds(TILES * g + t, 1), :].squeeze(1),
                                    start=(k == 0 and t == 0), stop=(k == 1 and t == TILES - 1))
                ins.then_inc(g_done, 1)

            pe.wait_ge(vb_ready, 1)
            pe.wait_ge(wT_copied, 1)
            transposes1(0, 0)
            transposes1(0, 1)
            pe.wait_ge(bias_ready, 1)
            pe.wait_ge(rep_copied, 2 * B)
            pe.wait_ge(ga_copied, B)
            qk_product(0, 0)
            pe.wait_ge(prod_step[0], SMALL)
            factors(1)
            pe.wait_ge(prod_step[1], SMALL)
            transposes1(1, 0)
            qk_product(0, 1)
            sums(0, 0)
            with pe.Fori(1, B - 1) as b:
                transposes1(b, 1)
                qk_product(b, 0)
                sums(b - 1, 1)
                transposes1(b + 1, 0)
                qk_product(b, 1)
                sums(b, 0)
            transposes1(B - 1, 1)
            qk_product(B - 1, 0)
            sums(B - 2, 1)
            qk_product(B - 1, 1)
            sums(B - 1, 0)
            sums(B - 1, 1)

            pe.wait_ge(g_saved, B)
            for b in range(B):
                ins = pe.transpose(bank[0][:, b * P:(b + 1) * P], gs[:, b, 0:D], ident[:, :])
            ins.then_inc(gT_mm, 1)
            for b in range(B):
                ins = pe.matmul(bank[1][0:1, b * P:(b + 1) * P], gs[:, b, D:D + 1], ident[:, :], start=True, stop=True)
            ins.then_inc(ks_mm, 1)
            pe.wait_ge(ks_diag_ready, 1)
            pe.wait_ge(phi_ready, 2 * GROUPS)
            pe.matmul(bank[2][:, :], ones[:, :], ks_diag[:, :, :], start=True, stop=True).then_inc(ksrep_mm, 1)
            pe.wait_ge(gT_saved, 1)
            pe.wait_ge(ks_saved, 1)
            for b in range(B):
                pe.matmul(bank[3][:, b * P:(b + 1) * P], wT[:, 2, :], gT[:, b, :], start=True, stop=False)
                ins = pe.matmul(bank[3][:, b * P:(b + 1) * P], vb_row[:, :], ks_row[:, b, :], start=False, stop=True)
            ins.then_inc(kv_mm, 1)
            pe.wait_ge(kv_saved, 1)
            for b in range(B):
                ins = pe.matmul(bank[4][:, b * P:(b + 1) * P], kvT[:, b, :], wT[:, 3, :], start=True, stop=True)
            ins.then_inc(m_mm, 1)

            def q_transposes(b, k):
                g = 2 * b + k
                pe.wait_ge(qn_ready, g + 1)
                used(pe, qT_ready, g)
                for t in range(TILES):
                    ins = pe.transpose(bank[0][:, t * P:(t + 1) * P], qn[:, k, t, :], ident[:, :])
                ins.then_inc(qnT_mm, 1)

            def attention(b, k):
                g = 2 * b + k
                pe.wait_ge(qT_ready, g + 1)
                used(pe, hs_ready, g)
                for t in range(TILES):
                    ins = pe.matmul(bank[1][:, t * P:(t + 1) * P], qT[:, k, t * P:(t + 1) * P],
                                    m_mat[:, bass.ds(b, 1), :].squeeze(1), start=True, stop=True)
                ins.then_inc(attn_mm, 1)

            def transposes3(b, k):
                g = 2 * b + k
                pe.wait_ge(n3_ready, g + 1)
                used(pe, h3T_ready, g)
                for t in range(TILES):
                    ins = pe.transpose(bank[2][:, t * P:(t + 1) * P], n3[:, k, t, :], ident[:, :])
                ins.then_inc(n3T_mm, 1)

            def up(b, k, c):
                g = 2 * b + k
                if c == 0:
                    pe.wait_ge(h3T_ready, g + 1)
                used(pe, gelu_done, CH * g + (0, -2, -1, 1)[c])
                pe.matmul(bank[3 + c % 3][:, :], w_up[:, c * P:(c + 1) * P], h3T[:, k, :],
                          start=True, stop=True).then_inc(up_mm, 1)

            def down(b, k, c):
                g = 2 * b + k
                pe.wait_ge(gelu_done, CH * g + c + 1)
                if c == 0:
                    used(pe, yT_ready, g)
                ins = pe.matmul(bank[6][:, :], w_down[:, c, :], act[:, k, c, :], start=(c == 0), stop=(c == CH - 1))
                if c == CH - 1:
                    ins.then_inc(down_mm, 1)

            def y_transposes(b, k):
                g = 2 * b + k
                pe.wait_ge(yT_ready, g + 1)
                used(pe, out_ready, g)
                for t in range(TILES):
                    ins = pe.transpose(bank[7][:, t * P:(t + 1) * P], yT[:, k, t * P:(t + 1) * P], ident[:, :])
                ins.then_inc(y_mm, 1)

            def step_b(b, k, attn=True, ffn=True, last=True):
                if attn:
                    q_transposes(b, k)
                if ffn:
                    transposes3(b - 1, k)
                if last:
                    down(b - 2 + k, 1 - k, 2)
                    down(b - 2 + k, 1 - k, 3)
                if attn:
                    attention(b, k)
                if ffn:
                    up(b - 1, k, 0)
                    up(b - 1, k, 1)
                if last:
                    y_transposes(b - 2 + k, 1 - k)
                if ffn:
                    up(b - 1, k, 2)
                    down(b - 1, k, 0)
                    up(b - 1, k, 3)
                    down(b - 1, k, 1)

            pe.wait_ge(m_saved, 1)
            pe.wait_ge(ksrep_saved, 1)
            step_b(0, 0, ffn=False, last=False)
            pe.wait_ge(ffn_in, 32)
            for c in range(CH):
                ins = pe.transpose(bank[3][:, c * P:(c + 1) * P], wexp_s[:, c * P:(c + 1) * P], ident[:, :])
            ins.then_inc(wexpT_mm, 1)
            pe.wait_ge(wexpT_saved, 1)
            pe.wait_ge(prod_step[0], NS)
            for c in range(CH):
                ins = pe.matmul(bank[4][:, :], wexpT[:, c, :], t_mat[0][:, c, :], start=(c == 0), stop=(c == CH - 1))
            ins.then_inc(wup_mm, 1)
            for ic in range(CH):
                for c in range(CH):
                    ins = pe.matmul(bank[5][:, ic:ic + 1], t_mat[0][:, c, ic * P:(ic + 1) * P], cols[:, 8 + c:9 + c],
                                    start=(c == 0), stop=(c == CH - 1))
            ins.then_inc(bup_mm, 1)
            step_b(0, 1, ffn=False, last=False)
            pe.wait_ge(prod_step[1], NS)
            for ic in range(CH):
                if ic >= 2:
                    pe.wait_ge(td_saved, ic - 1)
                for c in range(CH):
                    ins = pe.transpose(bank[6 + ic % 2][:, c * P:(c + 1) * P], t_mat[1][:, c, ic * P:(ic + 1) * P],
                                       ident[:, :])
                ins.then_inc(td_mm, 1)
            pe.wait_ge(td_saved, CH)
            for c in range(CH):
                for ic in range(CH):
                    ins = pe.matmul(bank[3][:, c * P:(c + 1) * P], t_down[:, ic, c * P:(c + 1) * P], wcon_s[:, ic, :],
                                    start=(ic == 0), stop=(ic == CH - 1))
            ins.then_inc(wdown_mm, 1)
            pe.wait_ge(wup_saved, 1)
            pe.wait_ge(wdown_saved, 1)
            pe.wait_ge(bup_saved, 1)
            step_b(1, 0, last=False)
            step_b(1, 1)
            with pe.Fori(2, B) as b:
                step_b(b, 0)
                step_b(b, 1)
            step_b(B, 0, attn=False)
            step_b(B, 1, attn=False)
            down(B - 1, 1, 2)
            down(B - 1, 1, 3)
            y_transposes(B - 1, 1)


_INS = ['L0_attn_input_tensor', 'L0_attn_Wq', 'L0_attn_bq', 'L0_attn_Wk', 'L0_attn_bk', 'L0_attn_Wv', 'L0_attn_bv',
        'L0_attn_Wd', 'L0_attn_bd', 'L0_attn_gamma', 'L0_attn_beta', 'L0_ffn_W_exp', 'L0_ffn_b_exp',
        'L0_ffn_up_weights', 'L0_ffn_up_bias', 'L0_ffn_down_weights', 'L0_ffn_W_con', 'L0_ffn_b_con',
        'L0_ffn_down_bias', 'L0_c', 'L0_wmod']
_OUTS = [((4, 1024, 128), 'float32')]


def kernel(**inputs):
    import numpy as _np
    import concourse.bacc as _bacc
    from concourse import mybir as _mybir
    from concourse.bass_utils import run_bass_kernel_spmd as _run

    nc = _bacc.Bacc("TRN2", target_bir_lowering=False, num_devices=1)
    arrays, args = {}, []
    for name in _INS:
        a = _np.ascontiguousarray(inputs[name])
        arrays[f"in_{name}_dram"] = a
        args.append(nc.dram_tensor(f"in_{name}_dram", a.shape, _mybir.dt.from_np(a.dtype), kind="ExternalInput").ap())
    for i, (shape, dtype) in enumerate(_OUTS):
        dt = _mybir.dt.from_np(_np.dtype(dtype))
        args.append(nc.dram_tensor(f"out_{i}_dram", shape, dt, kind="ExternalOutput").ap())
    adaln_block_kernel(nc, *args)
    r = _run(nc, [arrays], core_ids=[0])
    got = tuple(r.results[0][f"out_{i}_dram"] for i in range(len(_OUTS)))
    return got[0]
```

```python
from contextlib import ExitStack

import concourse.bass as bass
from concourse import mybir

ALU = mybir.AluOpType
ACT = mybir.ActivationFunctionType
AX_X = mybir.AxisListType.X
AX_XY = mybir.AxisListType.XY
F32 = mybir.dt.float32
BF16 = mybir.dt.bfloat16

P = 128
TILES = 4
LN_EPS = 1e-5
ATTN_LN_EPS = 1e-12
ATTN_EPS = 1e-6
GATE_FLOOR = 0.25


def adaln_block_kernel(nc, x_in, Wq, bq, Wk, bk, Wv, bv, Wd, bd, gamma, beta, W_exp, b_exp, up_w, up_bias,
                       down_w, W_con, b_con, down_bias, c_in, wmod, out):
    B, S, D = x_in.shape
    HID = W_exp.shape[1]
    CH = HID // P
    NS = up_w.shape[0]
    HEADS, HD = 16, D // 16
    GROUPS = B * S // (TILES * P)
    PER_B = GROUPS // B
    assert D == P and PER_B == 2 and CH == 4 and NS == 9 and GROUPS == 8
    SMALL = NS - 2

    x_v = x_in.rearrange("b (p j) d -> p b j d", p=P)
    out_v = out.rearrange("b (p j) d -> p b j d", p=P)

    with ExitStack() as ctx:
        def sb(name, shape, dt=F32):
            return ctx.enter_context(nc.sbuf_tensor(name, shape, dt))

        def sem(name):
            return ctx.enter_context(nc.semaphore(name))

        bank = [ctx.enter_context(nc.psum_tensor(f"bank{i}", [P, 512], F32)) for i in range(8)]

        x = sb("x", [P, B * 8, D])
        q = sb("q", [P, B * 8, D])
        r = sb("r", [P, B * 8, D + 1])
        mv1 = sb("mv1", [P, B * 8, 2])
        rs1 = sb("rs1", [P, B * 8])
        nb1 = sb("nb1", [P, B * 8])
        ve1 = sb("ve1", [P, B * 8])
        nm1 = sb("nm1", [P, B * 8])
        ident = sb("ident", [P, P])
        ones = sb("ones", [P, P])
        ones_bf = sb("ones_bf", [P, P], BF16)
        head_mask = sb("head_mask", [P, P])
        bits = sb("bits", [P, SMALL])
        nbits = sb("nbits", [P, SMALL])
        power = sb("power", [P, 8])
        eps1 = sb("eps1", [P, 8])
        eps23 = sb("eps23", [P, 8])
        c4 = sb("c4", [B, D])
        rows = sb("rows", [7, P])
        cols = sb("cols", [P, 7])
        bexp_s = sb("bexp_s", [P, CH])
        w_raw = sb("w_raw", [P, 4, P])
        wT = sb("wT", [P, 4, P])
        wmod_s = sb("wmod_s", [P, 6 * D])
        bias_1 = sb("bias_1", [P, 2])
        bias_h = sb("bias_h", [P, 2, 2], BF16)
        bias_p = sb("bias_p", [P, 2, 3])
        bias_f = sb("bias_f", [P, 2])
        bias3 = sb("bias3", [3, 2 * D], BF16)
        fb_row = sb("fb_row", [P, 2])
        bv_row = sb("bv_row", [1, D])
        vb_row = sb("vb_row", [1, D])
        bd_rep = sb("bd_rep", [P, D])
        gamma_rep = sb("gamma_rep", [P, D])
        beta_rep = sb("beta_rep", [P, D])
        sig = sb("sig", [P, 3, B])
        sc = sb("sc", [P, B])
        sc_rep = sb("sc_rep", [P, B, P])
        modc = sb("modc", [P, 6, B])
        gbw = sb("gbw", [P, 3, B])
        gbc = sb("gbc", [P, 2, B])
        bsum = sb("bsum", [P, 1])
        scale_rep = sb("scale_rep", [P, B, D])
        shift_rep = sb("shift_rep", [P, B, D])
        ga_rep = sb("ga_rep", [P, B, D])
        ga_sign = sb("ga_sign", [P, B, D])
        ga_abs = sb("ga_abs", [P, B, D])
        gg_rep = sb("gg_rep", [P, B, D])
        gbeta_rep = sb("gbeta_rep", [P, B, D])
        act = sb("act", [P, 2, CH, TILES * P])
        raw = act[:, :, :, :].rearrange("p i c n -> p i (c n)")
        prod = sb("prod", [P, 2, 2048])
        t_down = act[:, 1, :, :]
        h3T = prod[:, 1, 0:1024].rearrange("p (k n) -> p k n", k=2)
        fsel = sb("fsel", [P, 2, 1024])
        t_mat = sb("t_mat", [P, 2, CH, HID])
        wexp_s = sb("wexp_s", [P, HID])
        wexpT = sb("wexpT", [P, CH, D])
        wcon_s = sb("wcon_s", [P, CH, D])
        w_up = sb("w_up", [P, HID])
        w_down = sb("w_down", [P, CH, D])
        w_down_g = sb("w_down_g", [P, B, CH, D])
        gb_diag = sb("gb_diag", [P, B, D])
        gb_rep = sb("gb_rep", [P, B, D])
        fb_h = sb("fb_h", [P, 2, B], BF16)
        fb_f = sb("fb_f", [P, B])
        fb_p = sb("fb_p", [P, B, 3])
        fb3 = sb("fb3", [3, B, D], BF16)
        b_up = sb("b_up", [P, CH])
        bn1 = sb("bn1", [P, 2, TILES, 6])
        n1 = sb("n1", [P, 2, TILES, D])
        hT = sb("hT", [P, 2, TILES * P])
        e = sb("e", [P, 2, 512])
        ev = sb("ev", [P, 2, 512])
        kf = sb("kf", [P, 2, TILES, D])
        gs = sb("gs", [P, B, D + 1])
        gT = sb("gT", [P, B, D])
        ks_row = sb("ks_row", [1, B, D])
        ks_eps = sb("ks_eps", [P, B])
        ks_diag = sb("ks_diag", [P, B, D])
        ks_rep = sb("ks_rep", [P, B, D])
        kvT = sb("kvT", [P, B, D])
        m_mat = sb("m_mat", [P, B, D])
        qn, qT, n3 = n1, hT, kf
        qk = sb("qk", [P, TILES, D])
        den = sb("den", [P, TILES * HEADS])
        z = sb("z", [P, TILES * HEADS])
        hs = e[:, :, :].rearrange("p k (t d) -> p k t d", d=D)
        bn2 = sb("bn2", [P, TILES, 6])
        bn3 = sb("bn3", [P, TILES, 6])
        mv = sb("mv", [P, 2, 8, 2])
        ve = sb("ve", [P, 8])
        nm = sb("nm", [P, 8])
        rs = sb("rs", [P, 2, 8])
        nb = sb("nb", [P, 2, 8])
        nh = sb("nh", [P, 2, TILES, D])

        rows_in = sem("rows_in")
        c_ld = sem("c_ld")
        w_in = sem("w_in")
        wmod_in = sem("wmod_in")
        reps_in = sem("reps_in")
        bv_in = sem("bv_in")
        x_ld = [sem(f"x_ld{g}") for g in range(GROUPS)]
        bd_in = sem("bd_in")
        raw_in = [sem(f"raw_in{i}") for i in range(2)]
        ffn_in = sem("ffn_in")
        stored = sem("stored")
        const_ready = sem("const_ready")
        power_ready = sem("power_ready")
        bits_step = sem("bits_step")
        id_zero = sem("id_zero")
        id_ready = sem("id_ready")
        mask_step = sem("mask_step")
        cT_ready = sem("cT_ready")
        cols_ready = sem("cols_ready")
        cols_copied = sem("cols_copied")
        parts_mm = sem("parts_mm")
        wT_ready = sem("wT_ready")
        wT_copied = sem("wT_copied")
        silu_exp = sem("silu_exp")
        silu_step = sem("silu_step")
        sc_ready = sem("sc_ready")
        sc_rep_ready = sem("sc_rep_ready")
        modT_ready = sem("modT_ready")
        modc_step = sem("modc_step")
        modc_ready = sem("modc_ready")
        mod_rep = sem("mod_rep")
        rep_copied = sem("rep_copied")
        ga_copied = sem("ga_copied")
        gate_step = sem("gate_step")
        gate_ready = sem("gate_ready")
        gate_b = sem("gate_b")
        bias_step = sem("bias_step")
        bias_ready = sem("bias_ready")
        vb_mm = sem("vb_mm")
        vb_ready = sem("vb_ready")
        gates_mm = sem("gates_mm")
        fsel_step = sem("fsel_step")
        prod_step = [sem(f"prod_step{i}") for i in range(2)]
        t_ready = [sem(f"t_ready{i}") for i in range(2)]
        bn1_done = sem("bn1_done")
        ln1_stats = sem("ln1_stats")
        ln1_pool = sem("ln1_pool")
        ln1_scale = sem("ln1_scale")
        n1a_ready = sem("n1a_ready")
        n1v_ready = sem("n1v_ready")
        r_half = sem("r_half")
        r_ready = sem("r_ready")
        n1T_ready = sem("n1T_ready")
        hT_ready = sem("hT_ready")
        qk_ready = sem("qk_ready")
        relu_ready = sem("relu_ready")
        exp_ready = sem("exp_ready")
        phi_ready = sem("phi_ready")
        sums_done = sem("sums_done")
        g_saved = sem("g_saved")
        gT_mm = sem("gT_mm")
        gT_saved = sem("gT_saved")
        ks_mm = sem("ks_mm")
        ks_saved = sem("ks_saved")
        ks_eps_ready = sem("ks_eps_ready")
        ks_diag_ready = sem("ks_diag_ready")
        ksrep_mm = sem("ksrep_mm")
        ksrep_saved = sem("ksrep_saved")
        kv_mm = sem("kv_mm")
        kv_saved = sem("kv_saved")
        m_mm = sem("m_mm")
        m_saved = sem("m_saved")
        wexpT_mm = sem("wexpT_mm")
        wexpT_saved = sem("wexpT_saved")
        wup_mm = sem("wup_mm")
        wup_saved = sem("wup_saved")
        bup_mm = sem("bup_mm")
        bup_saved = sem("bup_saved")
        td_mm = sem("td_mm")
        td_saved = sem("td_saved")
        wdown_mm = sem("wdown_mm")
        wdown_saved = sem("wdown_saved")
        fb_step = sem("fb_step")
        fb_mm = sem("fb_mm")
        fb_ready = sem("fb_ready")
        gb_diag_ready = sem("gb_diag_ready")
        gb_mm = sem("gb_mm")
        gb_ready = sem("gb_ready")
        wdg_ready = sem("wdg_ready")
        qks_ready = sem("qks_ready")
        den_ready = sem("den_ready")
        z_ready = sem("z_ready")
        qn_ready = sem("qn_ready")
        qnT_mm = sem("qnT_mm")
        qT_ready = sem("qT_ready")
        attn_mm = sem("attn_mm")
        hs_ready = sem("hs_ready")
        bn2_done = sem("bn2_done")
        ln2_stats = sem("ln2_stats")
        bn3_done = sem("bn3_done")
        ln3_stats = sem("ln3_stats")
        ln_pool = sem("ln_pool")
        ln_scale = sem("ln_scale")
        nh_ready = sem("nh_ready")
        nhg_ready = sem("nhg_ready")
        xb_ready = sem("xb_ready")
        x1_ready = sem("x1_ready")
        n3a_ready = sem("n3a_ready")
        n3v_ready = sem("n3v_ready")
        n3T_mm = sem("n3T_mm")
        h3T_ready = sem("h3T_ready")
        up_mm = sem("up_mm")
        gelu_done = sem("gelu_done")
        down_mm = sem("down_mm")
        out_ready = sem("out_ready")

        def tiles(buf, g, w=D):
            return buf[:, bass.ds(g * TILES, TILES), 0:w]

        def used(eng, s, value):
            if not isinstance(value, int) or value > 0:
                eng.wait_ge(s, value)

        def apart(eng):
            eng.nop(nofuse=True)

        def bc(ap, shape):
            return ap.to_broadcast(shape)

        def per_tile(rep, b):
            return bc(rep[:, bass.ds(b, 1), :], [P, TILES, D])

        def region(t):
            return (8 * t, 8) if t < 2 else (4 * 2 ** t, 4 * 2 ** t)

        def products(eng, i, stages):
            def part(t):
                n = 2 ** (t + 1)
                if t == NS - 1:
                    return t_mat[:, i, :, :].rearrange("p c n -> p (c n)")
                return prod[:, i, 4 * n - 8:8 * n - 8]

            for t in stages:
                if t == 0:
                    w = raw[:, i, 0:8].rearrange("p (k o i) -> p k i o", k=2, o=2)
                    for k in range(2):
                        ins = eng.tensor_copy(part(0).rearrange("p (k i o) -> p k i o", k=2, i=2)[:, k], w[:, k])
                    ins.then_inc(prod_step[i], 1)
                elif t == 1:
                    eng.wait_ge(prod_step[i], 1)
                    w = raw[:, i, 8:16].rearrange("p (l o i) -> p i o l", o=2, i=2)
                    for h in range(2):
                        ins = eng.tensor_tensor(
                            part(1).rearrange("p (h c o l) -> p h c o l", h=2, c=2, o=2)[:, h],
                            bc(part(0).rearrange("p (h c l) -> p h c l", h=2, c=2)[:, h].unsqueeze(2), [P, 2, 2, 2]),
                            bc(w[:, h].unsqueeze(1), [P, 2, 2, 2]), ALU.mult)
                    ins.then_inc(prod_step[i], 1)
                else:
                    if t == 2:
                        eng.wait_ge(fsel_step, 2 * i + 2)
                    eng.wait_ge(prod_step[i], t)
                    eng.tensor_tensor(part(t).rearrange("p (c o l) -> p c o l", c=CH, o=2),
                                      bc(part(t - 1).rearrange("p (c l) -> p c l", c=CH).unsqueeze(2), [P, CH, 2, 2 ** t]),
                                      bc(fsel[:, i, 2 ** (t + 1):2 ** (t + 2)].rearrange("p (o l) -> p o l", o=2)
                                         .unsqueeze(1), [P, CH, 2, 2 ** t]),
                                      ALU.mult).then_inc(t_ready[i] if t == NS - 1 else prod_step[i], 1)

        block = ctx.enter_context(nc.Block())

        @block.sync
        def _(sp):
            sp.dma_start(x[:, 0:4, :], x_v[:, 0, 0:4, :]).then_inc(x_ld[0], 16)
            sp.dma_start(x[:, 4:8, :], x_v[:, 0, 4:8, :]).then_inc(x_ld[1], 16)
            for i, v in enumerate((bq, bk, bd)):
                sp.dma_start(rows[i:i + 1, :], v.rearrange("(a d) -> a d", a=1)).then_inc(rows_in, 16)
            sp.dma_start(rows[3:7, :], up_bias.rearrange("(a d) -> a d", d=P)).then_inc(rows_in, 16)
            sp.dma_start(bd_rep[:, :], bass.AP(tensor=bd.tensor, offset=bd.offset, ap=[[0, P], [1, D]])).then_inc(bd_in, 16)
            sp.dma_start(bv_row[:, :], bv.rearrange("(a d) -> a d", a=1)).then_inc(bv_in, 16)
            for g in range(2, GROUPS):
                h = g % 2 * 4
                sp.dma_start(x[:, 4 * g:4 * g + 4, :], x_v[:, g // 2, h:h + 4, :]).then_inc(x_ld[g], 16)
            for i, w in enumerate((up_w, down_w)):
                sp.dma_start(raw[:, i, 0:16].rearrange("p (t n) -> p t n", t=2),
                             bass.AP(tensor=w.tensor, offset=w.offset,
                                     ap=[[8, P], [2 * HID, 2], [1, 8]])).then_inc(raw_in[i], 16)
                for t in range(2, NS):
                    at, n = region(t)
                    src = bass.AP(tensor=w.tensor, offset=w.offset + t * HID * 2,
                                  ap=[[n, 2 ** (8 - t)], [0, 2 ** (t - 1)], [1, n]])
                    sp.dma_start(raw[:, i, at:at + n], src).then_inc(raw_in[i], 16)
                if i == 0:
                    sp.dma_start(wexp_s[:, :], W_exp).then_inc(ffn_in, 16)
            sp.dma_start(wcon_s[:, :, :], W_con.rearrange("(c p) d -> p c d", p=P)).then_inc(ffn_in, 16)
            sp.dma_start(bexp_s[:, :], b_exp.rearrange("(p c) -> p c", c=CH)).then_inc(ffn_in, 16)
            for i, v in enumerate((b_con, down_bias)):
                sp.dma_start(fb_row[:, i:i + 1], v.rearrange("(d a) -> d a", a=1)).then_inc(ffn_in, 16)
            for dst, v in ((gamma_rep, gamma), (beta_rep, beta)):
                sp.dma_start(dst[:, :], bass.AP(tensor=v.tensor, offset=v.offset,
                                                ap=[[0, P], [1, D]])).then_inc(reps_in, 16)

            def store(b, k):
                g = 2 * b + k
                sp.wait_ge(out_ready, g + 1)
                sp.dma_start(out_v[:, bass.ds(b, 1), 4 * k:4 * k + 4, :].squeeze(1),
                             tiles(x, g)).then_inc(stored, 16)

            with sp.Fori(0, B) as b:
                store(b, 0)
                store(b, 1)
            sp.wait_ge(stored, 16 * GROUPS)

        @block.gpsimd
        def _(pool):
            pool.memset(ident[:, :], 0.0).then_inc(id_zero, 1)
            pool.wait_ge(id_zero, 1)
            pool.affine_select(out=ident[:, :], in_=ident[:, :], compare_op=ALU.not_equal, fill=1.0, base=0,
                               pattern=[[-1, P]], channel_multiplier=1).then_inc(id_ready, 1)
            pool.memset(power[:, :], -0.5).then_inc(power_ready, 1)
            pool.memset(eps1[:, :], LN_EPS).then_inc(power_ready, 1)
            pool.memset(eps23[:, 0:4], ATTN_LN_EPS).then_inc(power_ready, 1)
            pool.memset(eps23[:, 4:8], LN_EPS).then_inc(power_ready, 1)
            pool.memset(ones[:, :], 1.0).then_inc(const_ready, 1)
            pool.memset(ones_bf[:, :], 1.0).then_inc(const_ready, 1)
            pool.memset(r[:, :, D:D + 1], 1.0).then_inc(const_ready, 1)

            def ln1(b):
                s = slice(8 * b, 8 * b + 8)
                pool.wait_ge(ln1_stats, 2 * b + 2)
                pool.tensor_tensor(ve1[:, s], mv1[:, s, 1], eps1[:, :], ALU.add).then_inc(ln1_pool, 1)
                pool.tensor_scalar(nm1[:, s], mv1[:, s, 0], -1.0, None, ALU.mult).then_inc(ln1_pool, 1)
                pool.wait_ge(ln1_pool, 3 * b + 2)
                pool.tensor_tensor(rs1[:, s], ve1[:, s], power[:, :], ALU.pow).then_inc(ln1_pool, 1)
                pool.wait_ge(ln1_pool, 3 * b + 3)
                pool.tensor_tensor(nb1[:, s], nm1[:, s], rs1[:, s], ALU.mult).then_inc(ln1_scale, 1)

            pool.wait_ge(power_ready, 4)
            ln1(0)
            pool.memset(head_mask[:, :], 1.0).then_inc(mask_step, 1)
            hm = head_mask[:, :].rearrange("p (h e) -> p h e", e=HD)
            pool.wait_ge(mask_step, 1)
            pool.affine_select(out=hm, in_=hm, compare_op=ALU.is_ge, fill=0.0, base=0,
                               pattern=[[-HD, HEADS], [0, HD]], channel_multiplier=1).then_inc(mask_step, 1)
            pool.wait_ge(mask_step, 2)
            pool.affine_select(out=hm, in_=hm, compare_op=ALU.is_ge, fill=0.0, base=HD - 1,
                               pattern=[[HD, HEADS], [0, HD]], channel_multiplier=-1).then_inc(mask_step, 1)

            ln1(1)
            pool.wait_ge(rep_copied, 2 * B)

            def step_a(b, k):
                g = 2 * b + k
                pool.wait_ge(n1a_ready, g + 1)
                pool.wait_ge(n1v_ready, g + 1)
                apart(pool)
                pool.tensor_tensor(tiles(r, g), n1[:, k, :, :], per_tile(scale_rep, b), ALU.mult).then_inc(r_half, 1)
                pool.wait_ge(r_half, g + 1)
                apart(pool)
                pool.tensor_tensor(tiles(r, g), tiles(r, g), per_tile(shift_rep, b), ALU.add).then_inc(r_ready, 1)

            step_a(0, 0)
            step_a(0, 1)
            ln1(2)
            step_a(1, 0)
            step_a(1, 1)
            ln1(3)
            with pool.Fori(2, B) as b:
                step_a(b, 0)
                step_a(b, 1)
            pool.wait_ge(raw_in[1], 16 * (NS - 1))
            products(pool, 1, range(NS))

            def divisor(b, k):
                g = 2 * b + k
                used(pool, den_ready, g)
                apart(pool)
                pool.tensor_tensor(qk[:, :, :], tiles(q, g), per_tile(ks_rep, b), ALU.mult).then_inc(qks_ready, 1)

            def step_b(b, k, attn=True, prev=True, more=True):
                g = 2 * b + k
                if prev:
                    bp = b - 1 + k
                    pool.wait_ge(nh_ready, g)
                    apart(pool)
                    pool.tensor_tensor(nh[:, 1 - k, :, :], nh[:, 1 - k, :, :], per_tile(gg_rep, bp),
                                       ALU.mult).then_inc(nhg_ready, 1)
                if more:
                    if k == 0:
                        divisor(b, 1)
                    else:
                        divisor(b + 1, 0)
                if attn:
                    pool.tensor_tensor(tiles(x, g), tiles(x, g), per_tile(gbeta_rep, b), ALU.add).then_inc(xb_ready, 1)
                lo, hi = (0 if attn else 4), (8 if prev else 4)
                if attn:
                    pool.wait_ge(ln2_stats, g + 1)
                if prev:
                    pool.wait_ge(ln3_stats, g)
                    used(pool, n3a_ready, g - 1)
                    used(pool, n3v_ready, g - 1)
                used(pool, nh_ready, g - 1)
                pool.tensor_tensor(ve[:, lo:hi], mv[:, k, lo:hi, 1], eps23[:, lo:hi], ALU.add).then_inc(ln_pool, 1)
                pool.tensor_scalar(nm[:, lo:hi], mv[:, k, lo:hi, 0], -1.0, None, ALU.mult).then_inc(ln_pool, 1)
                pool.wait_ge(ln_pool, 3 * g + 2)
                pool.tensor_tensor(rs[:, k, lo:hi], ve[:, lo:hi], power[:, lo:hi], ALU.pow).then_inc(ln_pool, 1)
                pool.wait_ge(ln_pool, 3 * g + 3)
                pool.tensor_tensor(nb[:, k, lo:hi], nm[:, lo:hi], rs[:, k, lo:hi], ALU.mult).then_inc(ln_scale, 1)

            pool.wait_ge(ksrep_saved, 1)
            divisor(0, 0)
            pool.wait_ge(gate_ready, 1)
            pool.wait_ge(reps_in, 32)
            for b in range(B):
                pool.tensor_tensor(gg_rep[:, b, :], ga_rep[:, b, :], gamma_rep[:, :], ALU.mult).then_inc(gate_step, 1)
                pool.tensor_tensor(gbeta_rep[:, b, :], ga_rep[:, b, :], beta_rep[:, :], ALU.mult).then_inc(gate_step, 1)
            pool.wait_ge(gate_step, 3 + 2 * B)
            step_b(0, 0, prev=False)
            step_b(0, 1)

            def gate_w_down(b):
                apart(pool)
                pool.tensor_tensor(w_down_g[:, bass.ds(b, 1), :, :].squeeze(1), w_down[:, :, :],
                                   bc(gb_rep[:, bass.ds(b, 1), :], [P, CH, D]), ALU.mult).then_inc(wdg_ready, 1)

            step_b(1, 0)
            pool.wait_ge(wdg_ready, 1)
            gate_w_down(1)
            step_b(1, 1)
            gate_w_down(2)
            with pool.Fori(2, B - 1) as b:
                step_b(b, 0)
                gate_w_down(b + 1)
                step_b(b, 1)
            step_b(B - 1, 0)
            step_b(B - 1, 1, more=False)
            step_b(B, 0, attn=False, more=False)

        @block.scalar
        def _(sc_e):
            sc_e.dma_start(c4[:, :], c_in).then_inc(c_ld, 16)
            sc_e.dma_start(wmod_s[:, :], wmod).then_inc(wmod_in, 16)
            sc_e.preload_act_table(ACT.Exp)
            sc_e.wait_ge(cT_ready, 1)
            sc_e.activation(sig[:, 0, :], bank[0][:, 0:B], ACT.Exp, scale=-1.0).then_inc(silu_exp, 1)
            for i, w in enumerate((Wq, Wk, Wv, Wd)):
                sc_e.dma_start(w_raw[:, i, :], w).then_inc(w_in, 16)
            sc_e.wait_ge(wT_ready, 1)
            sc_e.copy(wT[:, :, :], bank[1][:, :].rearrange("p (a b) -> p a b", a=4)).then_inc(wT_copied, 1)

            def norm1(b, k):
                g = 2 * b + k
                sc_e.wait_ge(ln1_scale, b + 1)
                used(sc_e, n1T_ready, g - 1)
                used(sc_e, r_half, g - 1)
                apart(sc_e)
                for t in range(2):
                    s = g * TILES + t
                    ins = sc_e.activation(n1[:, k, t, :], x[:, bass.ds(s, 1), :].squeeze(1), ACT.Identity,
                                          bias=nb1[:, bass.ds(s, 1)], scale=rs1[:, bass.ds(s, 1)])
                ins.then_inc(n1a_ready, 1)

            def shift_scale(b, k):
                g = 2 * b + k
                sc_e.wait_ge(n1T_ready, g + 1)
                used(sc_e, qk_ready, 2 * (g - 1))
                apart(sc_e)
                sc_e.activation(hT[:, k, :], bank[k][:, :], ACT.Identity, bias=modc[:, 0, bass.ds(b, 1)],
                                scale=modc[:, 1, bass.ds(b, 1)]).then_inc(hT_ready, 1)

            def exps(b, k):
                g = 2 * b + k
                for h in range(2):
                    sc_e.wait_ge(qk_ready, 2 * g + h + 1)
                    used(sc_e, phi_ready, 2 * (g - 1) + h + 1)
                    sc_e.activation(ev[:, h, :], bank[2 + 2 * k + h][:, :], ACT.Relu, bias=1.0,
                                    scale=-1.0).then_inc(relu_ready, 1)
                for h in range(2):
                    sc_e.wait_ge(relu_ready, 2 * g + h + 1)
                    sc_e.activation(e[:, h, :], ev[:, h, :], ACT.Exp, scale=-1.0).then_inc(exp_ready, 1)

            def step_a(b, k, norm=True):
                g = 2 * b + k
                shift_scale(b, k)
                if norm:
                    norm1(b + 1, k)
                if not isinstance(b, int) or g > 0:
                    exps(b - 1 + k, 1 - k)

            norm1(0, 0)
            norm1(0, 1)
            sc_e.wait_ge(modc_ready, 1)
            step_a(0, 0)
            sc_e.wait_ge(gates_mm, 2)
            for b in range(B):
                ins = sc_e.copy(ga_rep[:, b, :], bank[6 + b // 2][:, b % 2 * D:b % 2 * D + D])
                ins.then_inc(ga_copied, 1)
            sc_e.nop().then_inc(g_saved, 1)
            step_a(0, 1)
            with sc_e.Fori(1, B - 1) as b:
                step_a(b, 0)
                step_a(b, 1)
            step_a(B - 1, 0, norm=False)
            step_a(B - 1, 1, norm=False)
            sc_e.wait_ge(wexpT_mm, 1)
            sc_e.copy(wexpT[:, :, :], bank[7][:, :].rearrange("p (a b) -> p a b", a=CH)).then_inc(wexpT_saved, 1)
            exps(B - 1, 1)
            sc_e.preload_act_table(ACT.Gelu)

            def save_t_down(ic):
                sc_e.wait_ge(td_mm, ic + 1)
                sc_e.copy(t_down[:, ic, :].rearrange("q (p c) -> q c p", c=CH),
                          bank[7 - ic % 2][:, :].rearrange("q (c p) -> q c p", c=CH)).then_inc(td_saved, 1)

            sc_e.wait_ge(gT_mm, 1)
            sc_e.copy(gT[:, :, :], bank[2][:, :].rearrange("p (a b) -> p a b", a=B)).then_inc(gT_saved, 1)
            sc_e.wait_ge(ksrep_mm, 1)
            sc_e.copy(ks_rep[:, :, :], bank[4][:, :].rearrange("p (a b) -> p a b", a=B)).then_inc(ksrep_saved, 1)
            sc_e.wait_ge(m_mm, 1)
            sc_e.copy(m_mat[:, :, :], bank[2][:, :].rearrange("p (a b) -> p a b", a=B)).then_inc(m_saved, 1)

            def attn_T(b, k):
                g = 2 * b + k
                sc_e.wait_ge(qnT_mm, g + 1)
                used(sc_e, attn_mm, g - 1)
                sc_e.copy(qT[:, k, :], bank[0][:, :]).then_inc(qT_ready, 1)

            def norm2(b, k):
                g = 2 * b + k
                sc_e.wait_ge(ln_scale, g + 1)
                used(sc_e, x1_ready, g - 1)
                for t in range(TILES):
                    ins = sc_e.activation(nh[:, k, t, :], hs[:, k, t, :], ACT.Identity,
                                          bias=nb[:, k, t:t + 1], scale=rs[:, k, t:t + 1])
                ins.then_inc(nh_ready, 1)

            def ffn_in_T(b, k):
                g = 2 * b + k
                sc_e.wait_ge(n3T_mm, g + 1)
                used(sc_e, up_mm, CH * (g - 1))
                apart(sc_e)
                sc_e.activation(h3T[:, k, :], bank[2][:, :], ACT.Identity, bias=modc[:, 3, bass.ds(b, 1)],
                                scale=modc[:, 4, bass.ds(b, 1)]).then_inc(h3T_ready, 1)

            def gelu(b, k, c):
                g = 2 * b + k
                sc_e.wait_ge(up_mm, CH * g + c + 1)
                if c == 0:
                    used(sc_e, down_mm, g - 1)
                sc_e.activation(act[:, k, c, :], bank[3 + c % 3][:, :], ACT.Gelu,
                                bias=b_up[:, c:c + 1]).then_inc(gelu_done, 1)

            def norm3(b, k):
                g = 2 * b + k
                sc_e.wait_ge(ln_scale, g + 1)
                used(sc_e, n3T_mm, g - 2)
                apart(sc_e)
                for t in range(2):
                    ins = sc_e.activation(n3[:, 1 - k, t, :], x[:, bass.ds(TILES * (g - 1) + t, 1), :].squeeze(1),
                                          ACT.Identity, bias=nb[:, k, 4 + t:5 + t], scale=rs[:, k, 4 + t:5 + t])
                ins.then_inc(n3a_ready, 1)

            def step_b(b, k, attn=True, ffn=True, norm=True, more=True):
                if ffn:
                    ffn_in_T(b - 1, k)
                if ffn:
                    for c in range(CH - 1):
                        gelu(b - 1, k, c)
                if more:
                    attn_T(b + k, 1 - k)
                if attn:
                    norm2(b, k)
                if norm:
                    norm3(b, k)
                if ffn:
                    gelu(b - 1, k, CH - 1)

            attn_T(0, 0)
            for ic in range(CH):
                save_t_down(ic)
            attn_T(0, 1)
            norm2(0, 0)
            sc_e.wait_ge(wup_mm, 1)
            sc_e.copy(w_up[:, :], bank[4][:, :]).then_inc(wup_saved, 1)
            sc_e.wait_ge(gb_mm, 1)
            sc_e.copy(gb_rep[:, :, :], bank[2][:, :].rearrange("p (a b) -> p a b", a=B)).then_inc(gb_ready, 1)
            sc_e.wait_ge(fb_mm, 1)
            sc_e.copy(fb3[:, :, :], bank[7][0:3, :].rearrange("p (a b) -> p a b", a=B)).then_inc(fb_ready, 1)
            attn_T(1, 0)
            norm2(0, 1)
            norm3(0, 1)
            sc_e.wait_ge(wdown_mm, 1)
            sc_e.copy(w_down[:, :, :], bank[3][:, :].rearrange("p (a b) -> p a b", a=CH)).then_inc(wdown_saved, 1)
            sc_e.wait_ge(bup_saved, 1)
            step_b(1, 0)
            step_b(1, 1)
            with sc_e.Fori(2, B - 1) as b:
                step_b(b, 0)
                step_b(b, 1)
            step_b(B - 1, 0)
            step_b(B - 1, 1, more=False)
            step_b(B, 0, attn=False, more=False)
            step_b(B, 1, attn=False, norm=False, more=False)

        @block.vector
        def _(dve):
            def stats1(g):
                dve.wait_ge(x_ld[g], 16)
                used(dve, ln1_stats, g - 1)
                for t in range(TILES):
                    ins = dve.bn_stats(bn1[:, g % 2, t, :], x[:, g * TILES + t, :])
                ins.then_inc(bn1_done, 1)
                dve.wait_ge(bn1_done, g + 1)
                for t in range(TILES):
                    ins = dve.bn_aggr(mv1[:, g * TILES + t, :], bn1[:, g % 2, t, :])
                ins.then_inc(ln1_stats, 1)

            dve.wait_ge(id_ready, 1)
            for t in range(SMALL):
                v = ident[:, :].rearrange("p (a i l) -> p a i l", i=2, l=2 ** t)[:, :, 1, :]
                ins = dve.reduce_sum(bits[:, t:t + 1], v, AX_XY)
            ins.then_inc(bits_step, 1)
            dve.wait_ge(bits_step, 1)
            dve.tensor_scalar(nbits[:, :], bits[:, :], -1.0, 1.0, ALU.mult, ALU.add).then_inc(bits_step, 1)
            stats1(0)
            dve.wait_ge(silu_exp, 1)
            dve.tensor_scalar(sig[:, 1, :], sig[:, 0, :], 1.0, None, ALU.add).then_inc(silu_step, 1)
            dve.wait_ge(silu_step, 1)
            dve.reciprocal(sig[:, 2, :], sig[:, 1, :]).then_inc(silu_step, 1)
            dve.wait_ge(silu_step, 2)
            dve.tensor_tensor(sc[:, :], bank[0][:, 0:B], sig[:, 2, :], ALU.mult).then_inc(sc_ready, 1)
            dve.wait_ge(sc_ready, 1)
            dve.tensor_copy(sc_rep[:, :, :], bc(sc[:, :].unsqueeze(2), [P, B, P])).then_inc(sc_rep_ready, 1)
            stats1(1)
            dve.wait_ge(modT_ready, 1)
            dve.tensor_copy(modc[:, :, :], bank[5][:, 0:24].rearrange("p (j b) -> p j b", j=6)).then_inc(modc_step, 1)
            dve.wait_ge(modc_step, 1)
            for j in (1, 4):
                ins = dve.tensor_scalar(modc[:, j, :], modc[:, j, :], 1.0, None, ALU.add)
            ins.then_inc(modc_ready, 1)
            dve.wait_ge(cols_ready, 1)
            dve.tensor_copy(cols[:, :], bank[3][:, 0:7]).then_inc(cols_copied, 1)
            dve.wait_ge(cols_copied, 1)
            dve.tensor_scalar(bias_1[:, :], cols[:, 0:2], 1.0, None, ALU.add).then_inc(bias_step, 1)
            dve.wait_ge(bias_step, 1)
            dve.tensor_copy(bias_h[:, 0, :], bias_1[:, :]).then_inc(bias_step, 1)
            dve.wait_ge(bias_step, 2)
            dve.tensor_copy(bias_p[:, :, 0], bias_h[:, 0, :])
            dve.tensor_tensor(bias_f[:, :], bias_1[:, :], bias_h[:, 0, :], ALU.subtract).then_inc(bias_step, 1)
            dve.wait_ge(bias_step, 3)
            dve.tensor_copy(bias_h[:, 1, :], bias_f[:, :]).then_inc(bias_step, 1)
            dve.wait_ge(bias_step, 4)
            dve.tensor_copy(bias_p[:, :, 1], bias_h[:, 1, :])
            dve.tensor_tensor(bias_p[:, :, 2], bias_f[:, :], bias_h[:, 1, :], ALU.subtract).then_inc(bias_step, 1)

            def norm1(b, k):
                g = 2 * b + k
                dve.wait_ge(ln1_scale, b + 1)
                used(dve, n1T_ready, g - 1)
                used(dve, r_half, g - 1)
                apart(dve)
                for t in range(2, TILES):
                    s = g * TILES + t
                    ins = dve.tensor_scalar(n1[:, k, t, :], x[:, bass.ds(s, 1), :].squeeze(1),
                                            rs1[:, bass.ds(s, 1)], nb1[:, bass.ds(s, 1)], ALU.mult, ALU.add)
                ins.then_inc(n1v_ready, 1)

            norm1(0, 0)
            norm1(0, 1)
            stats1(2)
            stats1(3)
            dve.wait_ge(parts_mm, 1)
            dve.tensor_copy(bias3[:, :], bank[4][0:3, 0:2 * D]).then_inc(bias_ready, 1)
            dve.wait_ge(vb_mm, 1)
            dve.wait_ge(bv_in, 16)
            dve.tensor_tensor(vb_row[:, :], bv_row[:, :], bank[2][0:1, 0:D], ALU.subtract).then_inc(vb_ready, 1)
            dve.wait_ge(bd_in, 16)
            for b in range(B):
                dve.wait_ge(mod_rep, b // 2 + 1)
                m = bank[6 + b // 2][:, b % 2 * 2 * D:][:, 0:2 * D]
                dve.tensor_scalar(scale_rep[:, b, :], m[:, D:2 * D], 1.0, None, ALU.add).then_inc(rep_copied, 1)
                dve.tensor_tensor(shift_rep[:, b, :], m[:, 0:D], bd_rep[:, :], ALU.add).then_inc(rep_copied, 1)
            stats1(4)
            stats1(5)

            def weights(i, t, bit):
                at, n = region(t)
                return raw[:, bass.ds(i, 1), at:at + n].squeeze(1).rearrange("p (l o i) -> p i o l", o=2, i=2)[:, bit]

            def chosen(i, t):
                return fsel[:, bass.ds(i, 1), 2 ** (t + 1):2 ** (t + 2)].squeeze(1).rearrange("p (o l) -> p o l", o=2)

            def select_clear(i):
                for t in range(2, NS):
                    ins = dve.tensor_scalar(chosen(i, t), weights(i, t, 0), nbits[:, t - 2:t - 1], None, ALU.mult)
                ins.then_inc(fsel_step, 1)

            def select_set(i):
                dve.wait_ge(fsel_step, 2 * i + 1)
                apart(dve)
                for t in range(2, NS):
                    ins = dve.scalar_tensor_tensor(out=chosen(i, t), in0=weights(i, t, 1), scalar=bits[:, t - 2:t - 1],
                                                   in1=chosen(i, t), op0=ALU.mult, op1=ALU.add)
                ins.then_inc(fsel_step, 1)

            def phi(b, k):
                g = 2 * b + k
                dve.wait_ge(sums_done, g + 1)
                for h in range(2):
                    dve.wait_ge(exp_ready, 2 * g + h + 1)
                    em = e[:, h, :].rearrange("p (t w d) -> p t w d", t=2, w=2)
                    pv = bank[2 + 2 * k + h][:, :].rearrange("p (t w d) -> p t w d", t=2, w=2)
                    dve.tensor_tensor(kf[:, k, 2 * h:2 * h + 2, :], em[:, :, 1, :], pv[:, :, 1, :], ALU.max)
                    dve.tensor_tensor(q[:, bass.ds(TILES * g + 2 * h, 2), :], em[:, :, 0, :], pv[:, :, 0, :],
                                      ALU.max).then_inc(phi_ready, 1)

            def save_g(b):
                dve.wait_ge(sums_done, 2 * b + 4)
                dve.tensor_copy(gs[:, bass.ds(b, 1), :].squeeze(1), bank[6][:, 0:D + 1]).then_inc(g_saved, 1)

            def step_a(b, k, norm=True):
                g = 2 * b + k
                if norm:
                    norm1(b + 1, k)
                if not isinstance(b, int) or g > 0:
                    phi(b - 1 + k, 1 - k)

            step_a(0, 0)
            stats1(6)
            stats1(7)
            step_a(0, 1)
            for i in range(2):
                dve.wait_ge(raw_in[i], 16 * (NS - 1))
            with dve.Fori(1, B - 1) as b:
                step_a(b, 0)
                select_clear(b - 1)
                step_a(b, 1)
                select_set(b - 1)
                save_g(b - 1)
            step_a(B - 1, 0, norm=False)
            products(dve, 0, range(NS - 2))
            step_a(B - 1, 1, norm=False)
            save_g(B - 2)
            products(dve, 0, (NS - 2,))
            phi(B - 1, 1)
            save_g(B - 1)

            dve.wait_ge(g_saved, B + 1)
            dve.tensor_scalar(ks_eps[:, :], gs[:, :, D], ATTN_EPS, None, ALU.add).then_inc(ks_eps_ready, 1)
            dve.wait_ge(ks_eps_ready, 1)
            for b in range(B):
                ins = dve.tensor_scalar(ks_diag[:, b, :], ident[:, :], ks_eps[:, b:b + 1], None, ALU.mult)
            ins.then_inc(ks_diag_ready, 1)
            dve.wait_ge(ga_copied, B)
            dve.tensor_scalar(ga_sign[:, :, :], ga_rep[:, :, :], 0.0, 2.0, ALU.is_ge, ALU.mult).then_inc(gate_step, 1)
            dve.scalar_tensor_tensor(out=ga_abs[:, :, :], in0=ga_rep[:, :, :], scalar=-1.0, in1=ga_rep[:, :, :],
                                     op0=ALU.mult, op1=ALU.max).then_inc(gate_step, 1)
            dve.wait_ge(gate_step, 2)
            dve.tensor_scalar(ga_abs[:, :, :], ga_abs[:, :, :], GATE_FLOOR, None, ALU.max).then_inc(gate_step, 1)
            dve.wait_ge(gate_step, 3)
            dve.scalar_tensor_tensor(out=ga_rep[:, :, :], in0=ga_sign[:, :, :], scalar=-1.0, in1=ga_abs[:, :, :],
                                     op0=ALU.add, op1=ALU.mult).then_inc(gate_ready, 1)
            dve.wait_ge(ks_mm, 1)
            dve.tensor_copy(ks_row[:, :, :], bank[3][0:1, :].rearrange("p (a b) -> p a b", a=B)).then_inc(ks_saved, 1)
            dve.wait_ge(ffn_in, 80)
            dve.tensor_tensor(bsum[:, :], fb_row[:, 0:1], fb_row[:, 1:2], ALU.add).then_inc(gate_b, 1)
            dve.tensor_scalar(gbw[:, 0, :], modc[:, 5, :], 0.0, 2.0, ALU.is_ge, ALU.mult).then_inc(gate_b, 1)
            dve.scalar_tensor_tensor(out=gbw[:, 1, :], in0=modc[:, 5, :], scalar=-1.0, in1=modc[:, 5, :],
                                     op0=ALU.mult, op1=ALU.max).then_inc(gate_b, 1)
            dve.wait_ge(gate_b, 3)
            dve.tensor_scalar(gbw[:, 2, :], gbw[:, 1, :], GATE_FLOOR, None, ALU.max).then_inc(gate_b, 1)
            dve.wait_ge(gate_b, 4)
            dve.scalar_tensor_tensor(out=gbc[:, 0, :], in0=gbw[:, 0, :], scalar=-1.0, in1=gbw[:, 2, :],
                                     op0=ALU.add, op1=ALU.mult).then_inc(gate_b, 1)
            dve.wait_ge(gate_b, 5)
            dve.tensor_scalar(gbc[:, 1, :], gbc[:, 0, :], bsum[:, 0:1], None, ALU.mult).then_inc(gate_b, 1)
            dve.wait_ge(kv_mm, 1)
            dve.wait_ge(mask_step, 3)
            dve.tensor_tensor(kvT[:, :, :], bank[5][:, :].rearrange("p (a b) -> p a b", a=B),
                              bc(head_mask[:, :].unsqueeze(1), [P, B, P]), ALU.mult).then_inc(kv_saved, 1)

            def divide(b, k):
                g = 2 * b + k
                dve.wait_ge(qks_ready, g + 1)
                used(dve, z_ready, g)
                dve.reduce_sum(den[:, :], qk[:, :, :].rearrange("p t (h e) -> p (t h) e", e=HD), AX_X).then_inc(den_ready, 1)
                dve.wait_ge(den_ready, g + 1)
                used(dve, qn_ready, g)
                dve.reciprocal(z[:, :], den[:, :]).then_inc(z_ready, 1)
                dve.wait_ge(z_ready, g + 1)
                used(dve, qnT_mm, g - 1)
                dve.tensor_tensor(qn[:, k, :, :].rearrange("p t (h e) -> p (t h) e", e=HD),
                                  tiles(q, g).rearrange("p t (h e) -> p (t h) e", e=HD),
                                  bc(z[:, :].unsqueeze(2), [P, TILES * HEADS, HD]), ALU.mult).then_inc(qn_ready, 1)

            def step_b(b, k, attn=True, prev=True, more=True, final=True, norm=True):
                g = 2 * b + k
                if attn:
                    dve.wait_ge(attn_mm, g + 1)
                    dve.wait_ge(r_ready, g + 1)
                    used(dve, nh_ready, g - 1)
                    dve.tensor_tensor(hs[:, k, :, :], bank[1][:, :].rearrange("p (t d) -> p t d", t=TILES),
                                      tiles(r, g), ALU.add).then_inc(hs_ready, 1)
                    dve.wait_ge(hs_ready, g + 1)
                    used(dve, ln2_stats, g)
                    for t in range(TILES):
                        ins = dve.bn_stats(bn2[:, t, :], hs[:, k, t, :])
                    ins.then_inc(bn2_done, 1)
                    dve.wait_ge(bn2_done, g + 1)
                    for t in range(TILES):
                        ins = dve.bn_aggr(mv[:, k, t, :], bn2[:, t, :])
                    ins.then_inc(ln2_stats, 1)
                if prev:
                    dve.wait_ge(nhg_ready, g)
                    dve.wait_ge(xb_ready, g)
                    dve.tensor_tensor(tiles(x, g - 1), nh[:, 1 - k, :, :], tiles(x, g - 1), ALU.add).then_inc(x1_ready, 1)
                    dve.wait_ge(x1_ready, g)
                    used(dve, ln3_stats, g - 1)
                    for t in range(TILES):
                        ins = dve.bn_stats(bn3[:, t, :], x[:, bass.ds(TILES * (g - 1) + t, 1), :].squeeze(1))
                    ins.then_inc(bn3_done, 1)
                    dve.wait_ge(bn3_done, g)
                    for t in range(TILES):
                        ins = dve.bn_aggr(mv[:, k, 4 + t, :], bn3[:, t, :])
                    ins.then_inc(ln3_stats, 1)
                if more:
                    if k == 0:
                        divide(b, 1)
                    else:
                        divide(b + 1, 0)
                if final:
                    dve.wait_ge(down_mm, g - 2)
                    dve.tensor_tensor(tiles(x, g - 3), bank[7 - k][:, :].rearrange("p (t d) -> p t d", t=TILES),
                                      tiles(x, g - 3), ALU.add).then_inc(out_ready, 1)
                if norm:
                    dve.wait_ge(ln_scale, g + 1)
                    used(dve, n3T_mm, g - 2)
                    apart(dve)
                    for t in range(2, TILES):
                        ins = dve.tensor_scalar(n3[:, 1 - k, t, :], x[:, bass.ds(TILES * (g - 1) + t, 1), :].squeeze(1),
                                                rs[:, k, 4 + t:5 + t], nb[:, k, 4 + t:5 + t], ALU.mult, ALU.add)
                    ins.then_inc(n3v_ready, 1)

            divide(0, 0)
            dve.wait_ge(gate_b, 6)
            products(dve, 0, (NS - 1,))
            step_b(0, 0, prev=False, final=False, norm=False)
            dve.tensor_copy(fb_h[:, 0, :], gbc[:, 1, :]).then_inc(fb_step, 1)
            for b in range(B):
                ins = dve.tensor_scalar(gb_diag[:, b, :], ident[:, :], gbc[:, 0, b:b + 1], None, ALU.mult)
            ins.then_inc(gb_diag_ready, 1)
            dve.wait_ge(fb_step, 1)
            dve.tensor_copy(fb_p[:, :, 0], fb_h[:, 0, :])
            dve.tensor_tensor(fb_f[:, :], gbc[:, 1, :], fb_h[:, 0, :], ALU.subtract).then_inc(fb_step, 1)
            dve.wait_ge(fb_step, 2)
            dve.tensor_copy(fb_h[:, 1, :], fb_f[:, :]).then_inc(fb_step, 1)
            dve.wait_ge(fb_step, 3)
            dve.tensor_copy(fb_p[:, :, 1], fb_h[:, 1, :])
            dve.tensor_tensor(fb_p[:, :, 2], fb_f[:, :], fb_h[:, 1, :], ALU.subtract).then_inc(fb_step, 1)
            step_b(0, 1, final=False)
            dve.wait_ge(bup_mm, 1)
            dve.tensor_tensor(b_up[:, :], bank[5][:, 0:CH], cols[:, 3:7], ALU.add).then_inc(bup_saved, 1)
            step_b(1, 0, final=False)
            dve.wait_ge(gb_ready, 1)
            dve.wait_ge(wdown_saved, 1)
            dve.tensor_tensor(w_down_g[:, 0, :, :], w_down[:, :, :], bc(gb_rep[:, 0:1, :], [P, CH, D]),
                              ALU.mult).then_inc(wdg_ready, 1)
            step_b(1, 1)
            with dve.Fori(2, B - 1) as b:
                step_b(b, 0)
                step_b(b, 1)
            step_b(B - 1, 0)
            step_b(B - 1, 1, more=False)
            step_b(B, 0, attn=False, more=False)
            step_b(B, 1, attn=False, prev=False, more=False, norm=False)
            step_b(B + 1, 0, attn=False, prev=False, more=False, norm=False)

        @block.tensor
        def _(pe):
            pe.wait_ge(id_ready, 1)
            pe.wait_ge(c_ld, 16)
            pe.transpose(bank[0][:, 0:B], c4[:, :], ident[0:B, 0:B]).then_inc(cT_ready, 1)
            pe.wait_ge(wmod_in, 16)
            pe.wait_ge(sc_ready, 1)
            for j in range(6):
                ins = pe.matmul(bank[5][:, 4 * j:4 + 4 * j], wmod_s[:, j * D:(j + 1) * D], sc[:, :],
                                start=True, stop=True)
            ins.then_inc(modT_ready, 1)
            pe.wait_ge(sc_rep_ready, 1)

            def replicate_mod(h):
                for b in range(2):
                    ins = pe.matmul(bank[6 + h][:, b * 2 * D:(b + 1) * 2 * D], sc_rep[:, 2 * h + b, :],
                                    wmod_s[:, 0:2 * D], start=True, stop=True)
                ins.then_inc(mod_rep, 1)

            replicate_mod(0)
            pe.wait_ge(rows_in, 64)
            pe.transpose(bank[3][:, 0:7], rows[:, :], ident[0:7, 0:7]).then_inc(cols_ready, 1)
            pe.wait_ge(w_in, 64)
            for i in range(4):
                ins = pe.transpose(bank[1][:, i * P:(i + 1) * P], w_raw[:, i, :], ident[:, :])
            ins.then_inc(wT_ready, 1)

            def transposes1(b, k):
                g = 2 * b + k
                pe.wait_ge(n1a_ready, g + 1)
                pe.wait_ge(n1v_ready, g + 1)
                used(pe, hT_ready, g - 1)
                for t in range(TILES):
                    ins = pe.transpose(bank[k][:, t * P:(t + 1) * P], n1[:, k, t, :], ident[:, :])
                ins.then_inc(n1T_ready, 1)

            def qk_product(b, k):
                g = 2 * b + k
                pe.wait_ge(hT_ready, g + 1)
                for t in range(TILES):
                    if t % 2 == 0:
                        used(pe, phi_ready, 2 * (g - 2) + t // 2 + 1)
                    o = bank[2 + 2 * k + t // 2][:, t % 2 * 256:t % 2 * 256 + 256]
                    pe.matmul(o, ones_bf[0:3, :], bias3[:, :], start=True, stop=False)
                    ins = pe.matmul(o, hT[:, k, t * P:(t + 1) * P], wT[:, 0:2, :], start=False, stop=True)
                    if t % 2:
                        ins.then_inc(qk_ready, 1)

            def sums(b, k):
                g = 2 * b + k
                pe.wait_ge(phi_ready, 2 * g + 2)
                pe.wait_ge(r_ready, g + 1)
                if k == 0:
                    pe.wait_ge(g_saved, b + 1)
                for t in range(TILES):
                    ins = pe.matmul(bank[6][:, 0:D + 1], kf[:, k, t, :], r[:, bass.ds(TILES * g + t, 1), :].squeeze(1),
                                    start=(k == 0 and t == 0), stop=(k == 1 and t == TILES - 1))
                ins.then_inc(sums_done, 1)

            def step_a(b, k):
                g = 2 * b + k
                transposes1(b + k, 1 - k)
                qk_product(b, k)
                if not isinstance(b, int) or b > 0:
                    sums(b - 1, k)

            transposes1(0, 0)
            pe.wait_ge(bias_step, 5)
            for w in range(2):
                ins = pe.transpose(bank[4][0:3, w * D:(w + 1) * D], bias_p[:, w, :], ident[:, :])
            ins.then_inc(parts_mm, 1)
            pe.wait_ge(wT_copied, 1)
            transposes1(0, 1)
            pe.matmul(bank[2][0:1, 0:D], cols[:, 2:3], wT[:, 2, :], start=True, stop=True).then_inc(vb_mm, 1)
            replicate_mod(1)
            pe.wait_ge(bias_ready, 1)
            pe.wait_ge(vb_ready, 1)
            pe.wait_ge(const_ready, 3)
            qk_product(0, 0)
            pe.wait_ge(rep_copied, 2 * B)
            for h in range(2):
                for b in range(2):
                    ins = pe.matmul(bank[6 + h][:, b * D:(b + 1) * D], sc_rep[:, 2 * h + b, :], wmod_s[:, 2 * D:3 * D],
                                    start=True, stop=True)
                ins.then_inc(gates_mm, 1)
            pe.nop().then_inc(sums_done, 2)
            step_a(0, 1)
            with pe.Fori(1, B - 1) as b:
                step_a(b, 0)
                step_a(b, 1)
            step_a(B - 1, 0)
            pe.wait_ge(ffn_in, 80)
            pe.wait_ge(ga_copied, B)
            for c in range(CH):
                ins = pe.transpose(bank[7][:, c * P:(c + 1) * P],
                                   wexp_s[:, :].rearrange("d (p c) -> d c p", c=CH)[:, c], ident[:, :])
            ins.then_inc(wexpT_mm, 1)
            qk_product(B - 1, 1)
            sums(B - 2, 1)
            sums(B - 1, 0)
            sums(B - 1, 1)

            def t_down_transposes(ic):
                if ic < 2:
                    pe.wait_ge(wexpT_saved, 1)
                else:
                    pe.wait_ge(td_saved, ic - 1)
                for c in range(CH):
                    ins = pe.transpose(bank[7 - ic % 2][:, c * P:(c + 1) * P], t_mat[:, 1, c, ic * P:(ic + 1) * P],
                                       ident[:, :])
                ins.then_inc(td_mm, 1)

            pe.wait_ge(g_saved, B + 1)
            pe.wait_ge(phi_ready, 2 * GROUPS)
            for b in range(B):
                ins = pe.transpose(bank[2][:, b * P:(b + 1) * P], gs[:, b, 0:D], ident[:, :])
            ins.then_inc(gT_mm, 1)
            for b in range(B):
                ins = pe.matmul(bank[3][0:1, b * P:(b + 1) * P], gs[:, b, D:D + 1], ident[:, :], start=True, stop=True)
            ins.then_inc(ks_mm, 1)
            pe.wait_ge(ks_diag_ready, 1)
            pe.matmul(bank[4][:, :], ones[:, :], ks_diag[:, :, :], start=True, stop=True).then_inc(ksrep_mm, 1)
            pe.wait_ge(gT_saved, 1)
            pe.wait_ge(ks_saved, 1)
            for b in range(B):
                pe.matmul(bank[5][:, b * P:(b + 1) * P], wT[:, 2, :], gT[:, b, :], start=True, stop=False)
                ins = pe.matmul(bank[5][:, b * P:(b + 1) * P], vb_row[:, :], ks_row[:, b, :], start=False, stop=True)
            ins.then_inc(kv_mm, 1)
            pe.wait_ge(kv_saved, 1)
            for b in range(B):
                ins = pe.matmul(bank[2][:, b * P:(b + 1) * P], kvT[:, b, :], wT[:, 3, :], start=True, stop=True)
            ins.then_inc(m_mm, 1)

            def q_transposes(b, k):
                g = 2 * b + k
                pe.wait_ge(qn_ready, g + 1)
                used(pe, qT_ready, g)
                for t in range(TILES):
                    ins = pe.transpose(bank[0][:, t * P:(t + 1) * P], qn[:, k, t, :], ident[:, :])
                ins.then_inc(qnT_mm, 1)

            def attention(b, k):
                g = 2 * b + k
                pe.wait_ge(qT_ready, g + 1)
                used(pe, hs_ready, g)
                for t in range(TILES):
                    ins = pe.matmul(bank[1][:, t * P:(t + 1) * P], qT[:, k, t * P:(t + 1) * P],
                                    m_mat[:, bass.ds(b, 1), :].squeeze(1), start=True, stop=True)
                ins.then_inc(attn_mm, 1)

            def transposes3(b, k):
                g = 2 * b + k
                pe.wait_ge(n3a_ready, g + 1)
                pe.wait_ge(n3v_ready, g + 1)
                used(pe, h3T_ready, g)
                for t in range(TILES):
                    ins = pe.transpose(bank[2][:, t * P:(t + 1) * P], n3[:, k, t, :], ident[:, :])
                ins.then_inc(n3T_mm, 1)

            def up(b, k, c):
                g = 2 * b + k
                if c == 0:
                    pe.wait_ge(h3T_ready, g + 1)
                used(pe, gelu_done, CH * g + (0, -2, -1, 1)[c])
                pe.matmul(bank[3 + c % 3][:, :], w_up[:, c * P:(c + 1) * P], h3T[:, k, :],
                          start=True, stop=True).then_inc(up_mm, 1)

            def down(b, k, c):
                g = 2 * b + k
                if c == 0:
                    used(pe, out_ready, g - 1)
                    pe.wait_ge(wdg_ready, b + 1)
                    apart(pe)
                    pe.matmul(bank[6 + k][:, :], ones_bf[0:3, :], bc(fb3[:, bass.ds(b, 1), :], [3, TILES, D]),
                              start=True, stop=False, skip_group_check=True)
                pe.wait_ge(gelu_done, CH * g + c + 1)
                apart(pe)
                for t in range(TILES):
                    ins = pe.matmul(bank[6 + k][:, t * P:(t + 1) * P], act[:, k, c, t * P:(t + 1) * P],
                                    w_down_g[:, bass.ds(b, 1), c, :].squeeze(1), start=False, stop=(c == CH - 1),
                                    skip_group_check=True)
                if c == CH - 1:
                    ins.then_inc(down_mm, 1)

            def step_b(b, k, last=True, more=True):
                if last:
                    down(b - 2 + k, 1 - k, 2)
                transposes3(b - 1, k)
                if last:
                    down(b - 2 + k, 1 - k, 3)
                up(b - 1, k, 0)
                up(b - 1, k, 1)
                up(b - 1, k, 2)
                down(b - 1, k, 0)
                if more:
                    q_transposes(b + k, 1 - k)
                up(b - 1, k, 3)
                if more:
                    attention(b + k, 1 - k)
                down(b - 1, k, 1)

            q_transposes(0, 0)
            pe.wait_ge(t_ready[1], 1)
            t_down_transposes(0)
            t_down_transposes(1)
            pe.wait_ge(m_saved, 1)
            attention(0, 0)
            t_down_transposes(2)
            t_down_transposes(3)
            pe.wait_ge(t_ready[0], 1)
            pe.wait_ge(ksrep_saved, 1)
            for c in range(CH):
                ins = pe.matmul(bank[4][:, :], wexpT[:, c, :], t_mat[:, 0, c, :], start=(c == 0), stop=(c == CH - 1))
            ins.then_inc(wup_mm, 1)
            q_transposes(0, 1)
            attention(0, 1)
            for ic in range(CH):
                for c in range(CH):
                    ins = pe.matmul(bank[5][:, ic:ic + 1], t_mat[:, 0, c, ic * P:(ic + 1) * P], bexp_s[:, c:c + 1],
                                    start=(c == 0), stop=(c == CH - 1))
            ins.then_inc(bup_mm, 1)
            pe.wait_ge(gb_diag_ready, 1)
            pe.wait_ge(m_saved, 1)
            pe.matmul(bank[2][:, :], ones[:, :], gb_diag[:, :, :], start=True, stop=True).then_inc(gb_mm, 1)
            pe.wait_ge(fb_step, 4)
            pe.wait_ge(td_saved, CH)
            for b in range(B):
                ins = pe.transpose(bank[7][0:3, b * P:(b + 1) * P], fb_p[:, b, :], ident[:, :])
            ins.then_inc(fb_mm, 1)
            pe.wait_ge(td_saved, CH)
            q_transposes(1, 0)

            def w_down_product(c):
                for ic in range(CH):
                    ins = pe.matmul(bank[3][:, c * P:(c + 1) * P], t_down[:, ic, c * P:(c + 1) * P], wcon_s[:, ic, :],
                                    start=(ic == 0), stop=(ic == CH - 1))
                return ins

            w_down_product(0)
            attention(1, 0)
            w_down_product(1)
            w_down_product(2)
            w_down_product(3).then_inc(wdown_mm, 1)
            pe.wait_ge(wup_saved, 1)
            pe.wait_ge(bup_saved, 1)
            pe.wait_ge(wdown_saved, 1)
            pe.wait_ge(fb_ready, 1)
            step_b(1, 0, last=False)
            step_b(1, 1)
            with pe.Fori(2, B - 1) as b:
                step_b(b, 0)
                step_b(b, 1)
            step_b(B - 1, 0)
            step_b(B - 1, 1, more=False)
            step_b(B, 0, more=False)
            step_b(B, 1, more=False)
            down(B - 1, 1, 2)
            down(B - 1, 1, 3)


_INS = ['L0_attn_input_tensor', 'L0_attn_Wq', 'L0_attn_bq', 'L0_attn_Wk', 'L0_attn_bk', 'L0_attn_Wv', 'L0_attn_bv',
        'L0_attn_Wd', 'L0_attn_bd', 'L0_attn_gamma', 'L0_attn_beta', 'L0_ffn_W_exp', 'L0_ffn_b_exp',
        'L0_ffn_up_weights', 'L0_ffn_up_bias', 'L0_ffn_down_weights', 'L0_ffn_W_con', 'L0_ffn_b_con',
        'L0_ffn_down_bias', 'L0_c', 'L0_wmod']
_OUTS = [((4, 1024, 128), 'float32')]


def kernel(**inputs):
    import numpy as _np
    import concourse.bacc as _bacc
    from concourse import mybir as _mybir
    from concourse.bass_utils import run_bass_kernel_spmd as _run

    nc = _bacc.Bacc("TRN2", target_bir_lowering=False, num_devices=1)
    arrays, args = {}, []
    for name in _INS:
        a = _np.ascontiguousarray(inputs[name])
        arrays[f"in_{name}_dram"] = a
        args.append(nc.dram_tensor(f"in_{name}_dram", a.shape, _mybir.dt.from_np(a.dtype), kind="ExternalInput").ap())
    for i, (shape, dtype) in enumerate(_OUTS):
        dt = _mybir.dt.from_np(_np.dtype(dtype))
        args.append(nc.dram_tensor(f"out_{i}_dram", shape, dt, kind="ExternalOutput").ap())
    adaln_block_kernel(nc, *args)
    r = _run(nc, [arrays], core_ids=[0])
    got = tuple(r.results[0][f"out_{i}_dram"] for i in range(len(_OUTS)))
    return got[0]
```

```python
from contextlib import ExitStack

import concourse.bass as bass
from concourse import mybir

ALU = mybir.AluOpType
ACT = mybir.ActivationFunctionType
AX_X = mybir.AxisListType.X
AX_XY = mybir.AxisListType.XY
F32 = mybir.dt.float32
BF16 = mybir.dt.bfloat16

P = 128
TILES = 4
LN_EPS = 1e-5
ATTN_LN_EPS = 1e-12
ATTN_EPS = 1e-6
GATE_FLOOR = 0.25


def adaln_block_kernel(nc, x_in, Wq, bq, Wk, bk, Wv, bv, Wd, bd, gamma, beta, W_exp, b_exp, up_w, up_bias,
                       down_w, W_con, b_con, down_bias, c_in, wmod, out):
    B, S, D = x_in.shape
    HID = W_exp.shape[1]
    CH = HID // P
    NS = up_w.shape[0]
    HEADS, HD = 16, D // 16
    GROUPS = B * S // (TILES * P)
    PER_B = GROUPS // B
    assert D == P and PER_B == 2 and CH == 4 and NS == 9 and GROUPS == 8
    SMALL = NS - 2

    x_v = x_in.rearrange("b (p j) d -> p b j d", p=P)
    out_v = out.rearrange("b (p j) d -> p b j d", p=P)

    with ExitStack() as ctx:
        def sb(name, shape, dt=F32):
            return ctx.enter_context(nc.sbuf_tensor(name, shape, dt))

        def sem(name):
            return ctx.enter_context(nc.semaphore(name))

        bank = [ctx.enter_context(nc.psum_tensor(f"bank{i}", [P, 512], F32)) for i in range(8)]

        x = sb("x", [P, B * 8, D])
        q = sb("q", [P, B * 8, D])
        r = sb("r", [P, B * 8, D + 1])
        mv1 = sb("mv1", [P, B * 8, 2])
        rs1 = sb("rs1", [P, B * 8])
        nb1 = sb("nb1", [P, B * 8])
        ve1 = sb("ve1", [P, B * 8])
        nm1 = sb("nm1", [P, B * 8])
        ident = sb("ident", [P, P])
        ones = sb("ones", [P, P])
        ones_bf = sb("ones_bf", [P, P], BF16)
        head_mask = sb("head_mask", [P, P])
        bits = sb("bits", [P, SMALL])
        nbits = sb("nbits", [P, SMALL])
        power = sb("power", [P, 8])
        eps1 = sb("eps1", [P, 8])
        eps23 = sb("eps23", [P, 8])
        c4 = sb("c4", [B, D])
        rows = sb("rows", [7, P])
        cols = sb("cols", [P, 7])
        bexp_s = sb("bexp_s", [P, CH])
        w_raw = sb("w_raw", [P, 4, P])
        wT = sb("wT", [P, 4, P])
        wmod_s = sb("wmod_s", [P, 6 * D])
        bias_1 = sb("bias_1", [P, 2 + B])
        bias_h = sb("bias_h", [P, 2, 2 + B], BF16)
        bias_p = sb("bias_p", [P, 2 + B, 3])
        bias_f = sb("bias_f", [P, 2 + B])
        bias3 = sb("bias3", [3, 2 * D], BF16)
        fb_row = sb("fb_row", [P, 2])
        bv_row = sb("bv_row", [1, D])
        vb_row = sb("vb_row", [1, B, D])
        sh3 = sb("sh3", [3, B, D], BF16)
        gamma_rep = sb("gamma_rep", [P, D])
        beta_rep = sb("beta_rep", [P, D])
        sig = sb("sig", [P, 3, B])
        sc = sb("sc", [P, B])
        sc_rep = sb("sc_rep", [P, B, P])
        modc = sb("modc", [P, 6, B])
        gbw = sb("gbw", [P, 3, B])
        gbc = sb("gbc", [P, 2, B])
        bsum = sb("bsum", [P, 1])
        scale_rep = sb("scale_rep", [P, B, D])
        ga_rep = sb("ga_rep", [P, B, D])
        ga_sign = sb("ga_sign", [P, B, D])
        ga_abs = sb("ga_abs", [P, B, D])
        gg_rep = sb("gg_rep", [P, B, D])
        gbeta_rep = sb("gbeta_rep", [P, B, D])
        act = sb("act", [P, 2, CH, TILES * P])
        raw = act[:, :, :, :].rearrange("p i c n -> p i (c n)")
        prod = sb("prod", [P, 2, 2048])
        t_down = act[:, 1, :, :]
        h3T = prod[:, 1, 0:1024].rearrange("p (k n) -> p k n", k=2)
        fsel = sb("fsel", [P, 2, 1024])
        t_mat = sb("t_mat", [P, 2, CH, HID])
        wexp_s = sb("wexp_s", [P, HID])
        wexpT = sb("wexpT", [P, CH, D])
        wcon_s = sb("wcon_s", [P, CH, D])
        w_up = sb("w_up", [P, HID])
        w_down = sb("w_down", [P, CH, D])
        w_down_g = sb("w_down_g", [P, B, CH, D])
        gb_diag = sb("gb_diag", [P, B, D])
        gb_rep = sb("gb_rep", [P, B, D])
        fb_h = sb("fb_h", [P, 2, B], BF16)
        fb_f = sb("fb_f", [P, B])
        fb_p = sb("fb_p", [P, B, 3])
        fb3 = sb("fb3", [3, B, D], BF16)
        b_up = sb("b_up", [P, CH])
        bn1 = sb("bn1", [P, 2, TILES, 6])
        n1 = sb("n1", [P, 2, TILES, D])
        hT = sb("hT", [P, 2, TILES * P])
        e = sb("e", [P, 2, 512])
        ev = sb("ev", [P, 2, 512])
        kf = sb("kf", [P, 2, TILES, D])
        gs = sb("gs", [P, B, D + 1])
        gT = sb("gT", [P, B, D])
        ks_row = sb("ks_row", [1, B, D])
        ks_eps = sb("ks_eps", [P, B])
        ks_diag = sb("ks_diag", [P, B, D])
        ks_rep = sb("ks_rep", [P, B, D])
        kvT = sb("kvT", [P, B, D])
        m_mat = sb("m_mat", [P, B, D])
        qn, qT, n3 = n1, hT, kf
        qk = sb("qk", [P, TILES, D])
        den = sb("den", [P, TILES * HEADS])
        z = sb("z", [P, TILES * HEADS])
        hs = e[:, :, :].rearrange("p k (t d) -> p k t d", d=D)
        bn2 = sb("bn2", [P, TILES, 6])
        bn3 = sb("bn3", [P, TILES, 6])
        mv = sb("mv", [P, 2, 8, 2])
        ve = sb("ve", [P, 8])
        nm = sb("nm", [P, 8])
        rs = sb("rs", [P, 2, 8])
        nb = sb("nb", [P, 2, 8])
        nh = sb("nh", [P, 2, TILES, D])

        rows_in = sem("rows_in")
        c_ld = sem("c_ld")
        w_in = sem("w_in")
        wmod_in = sem("wmod_in")
        reps_in = sem("reps_in")
        bv_in = sem("bv_in")
        x_ld = [sem(f"x_ld{g}") for g in range(GROUPS)]
        raw_in = [sem(f"raw_in{i}") for i in range(2)]
        ffn_in = sem("ffn_in")
        stored = sem("stored")
        const_ready = sem("const_ready")
        power_ready = sem("power_ready")
        bits_step = sem("bits_step")
        id_zero = sem("id_zero")
        id_ready = sem("id_ready")
        mask_step = sem("mask_step")
        cT_ready = sem("cT_ready")
        cols_ready = sem("cols_ready")
        cols_copied = sem("cols_copied")
        parts_mm = sem("parts_mm")
        wT_ready = sem("wT_ready")
        wT_copied = sem("wT_copied")
        silu_exp = sem("silu_exp")
        silu_step = sem("silu_step")
        sc_ready = sem("sc_ready")
        sc_rep_ready = sem("sc_rep_ready")
        modT_ready = sem("modT_ready")
        modc_step = sem("modc_step")
        modc_ready = sem("modc_ready")
        mod_rep = sem("mod_rep")
        rep_copied = sem("rep_copied")
        ga_copied = sem("ga_copied")
        gate_step = sem("gate_step")
        gate_ready = sem("gate_ready")
        gate_b = sem("gate_b")
        bias_step = sem("bias_step")
        bias_ready = sem("bias_ready")
        vb_mm = sem("vb_mm")
        vb_ready = sem("vb_ready")
        sh_mm = sem("sh_mm")
        sh_ready = sem("sh_ready")
        gates_mm = sem("gates_mm")
        fsel_step = sem("fsel_step")
        prod_step = [sem(f"prod_step{i}") for i in range(2)]
        t_ready = [sem(f"t_ready{i}") for i in range(2)]
        ahead_step = sem("ahead_step")
        ahead_scale = sem("ahead_scale")
        bn1_done = sem("bn1_done")
        ln1_stats = sem("ln1_stats")
        ln1_pool = sem("ln1_pool")
        ln1_scale = sem("ln1_scale")
        n1a_ready = sem("n1a_ready")
        n1v_ready = sem("n1v_ready")
        r_ready = sem("r_ready")
        n1T_ready = sem("n1T_ready")
        hT_ready = sem("hT_ready")
        qk_ready = sem("qk_ready")
        relu_ready = sem("relu_ready")
        exp_ready = sem("exp_ready")
        phi_ready = sem("phi_ready")
        sums_done = sem("sums_done")
        g_saved = sem("g_saved")
        gT_mm = sem("gT_mm")
        gT_saved = sem("gT_saved")
        ks_mm = sem("ks_mm")
        ks_saved = sem("ks_saved")
        ks_eps_ready = sem("ks_eps_ready")
        ks_diag_ready = sem("ks_diag_ready")
        ksrep_mm = sem("ksrep_mm")
        ksrep_saved = sem("ksrep_saved")
        kv_mm = sem("kv_mm")
        kv_saved = sem("kv_saved")
        m_mm = sem("m_mm")
        m_saved = sem("m_saved")
        wexpT_mm = sem("wexpT_mm")
        wexpT_saved = sem("wexpT_saved")
        wup_mm = sem("wup_mm")
        wup_saved = sem("wup_saved")
        bup_mm = sem("bup_mm")
        bup_saved = sem("bup_saved")
        td_mm = sem("td_mm")
        td_saved = sem("td_saved")
        wdown_mm = sem("wdown_mm")
        wdown_saved = sem("wdown_saved")
        fb_step = sem("fb_step")
        fb_mm = sem("fb_mm")
        fb_ready = sem("fb_ready")
        gb_diag_ready = sem("gb_diag_ready")
        gb_mm = sem("gb_mm")
        gb_ready = sem("gb_ready")
        wdg_ready = sem("wdg_ready")
        qks_ready = sem("qks_ready")
        den_ready = sem("den_ready")
        z_ready = sem("z_ready")
        qn_ready = sem("qn_ready")
        qnT_mm = sem("qnT_mm")
        qT_ready = sem("qT_ready")
        attn_mm = sem("attn_mm")
        hs_ready = sem("hs_ready")
        bn2_done = sem("bn2_done")
        ln2_stats = sem("ln2_stats")
        bn3_done = sem("bn3_done")
        ln3_stats = sem("ln3_stats")
        ln_pool = sem("ln_pool")
        ln_scale = sem("ln_scale")
        nh_ready = sem("nh_ready")
        nhg_ready = sem("nhg_ready")
        xb_ready = sem("xb_ready")
        x1_ready = sem("x1_ready")
        n3a_ready = sem("n3a_ready")
        n3v_ready = sem("n3v_ready")
        n3T_mm = sem("n3T_mm")
        h3T_ready = sem("h3T_ready")
        up_mm = sem("up_mm")
        gelu_done = sem("gelu_done")
        down_mm = sem("down_mm")
        out_ready = sem("out_ready")

        def tiles(buf, g, w=D):
            return buf[:, bass.ds(g * TILES, TILES), 0:w]

        def used(eng, s, value):
            if not isinstance(value, int) or value > 0:
                eng.wait_ge(s, value)

        def apart(eng):
            eng.nop(nofuse=True)

        def bc(ap, shape):
            return ap.to_broadcast(shape)

        def per_tile(rep, b):
            return bc(rep[:, bass.ds(b, 1), :], [P, TILES, D])

        def region(t):
            return (8 * t, 8) if t < 2 else (4 * 2 ** t, 4 * 2 ** t)

        def products(eng, i, stages):
            def part(t):
                n = 2 ** (t + 1)
                if t == NS - 1:
                    return t_mat[:, i, :, :].rearrange("p c n -> p (c n)")
                return prod[:, i, 4 * n - 8:8 * n - 8]

            for t in stages:
                if t == 0:
                    w = raw[:, i, 0:8].rearrange("p (k o i) -> p k i o", k=2, o=2)
                    for k in range(2):
                        ins = eng.tensor_copy(part(0).rearrange("p (k i o) -> p k i o", k=2, i=2)[:, k], w[:, k])
                    ins.then_inc(prod_step[i], 1)
                elif t == 1:
                    eng.wait_ge(prod_step[i], 1)
                    w = raw[:, i, 8:16].rearrange("p (l o i) -> p i o l", o=2, i=2)
                    for h in range(2):
                        ins = eng.tensor_tensor(
                            part(1).rearrange("p (h c o l) -> p h c o l", h=2, c=2, o=2)[:, h],
                            bc(part(0).rearrange("p (h c l) -> p h c l", h=2, c=2)[:, h].unsqueeze(2), [P, 2, 2, 2]),
                            bc(w[:, h].unsqueeze(1), [P, 2, 2, 2]), ALU.mult)
                    ins.then_inc(prod_step[i], 1)
                else:
                    if t == 2:
                        eng.wait_ge(fsel_step, 2 * i + 2)
                    eng.wait_ge(prod_step[i], t)
                    eng.tensor_tensor(part(t).rearrange("p (c o l) -> p c o l", c=CH, o=2),
                                      bc(part(t - 1).rearrange("p (c l) -> p c l", c=CH).unsqueeze(2), [P, CH, 2, 2 ** t]),
                                      bc(fsel[:, i, 2 ** (t + 1):2 ** (t + 2)].rearrange("p (o l) -> p o l", o=2)
                                         .unsqueeze(1), [P, CH, 2, 2 ** t]),
                                      ALU.mult).then_inc(t_ready[i] if t == NS - 1 else prod_step[i], 1)

        block = ctx.enter_context(nc.Block())

        @block.sync
        def _(sp):
            sp.dma_start(x[:, 0:4, :], x_v[:, 0, 0:4, :]).then_inc(x_ld[0], 16)
            sp.dma_start(x[:, 4:8, :], x_v[:, 0, 4:8, :]).then_inc(x_ld[1], 16)
            for i, v in enumerate((bq, bk, bd)):
                sp.dma_start(rows[i:i + 1, :], v.rearrange("(a d) -> a d", a=1)).then_inc(rows_in, 16)
            sp.dma_start(rows[3:7, :], up_bias.rearrange("(a d) -> a d", d=P)).then_inc(rows_in, 16)
            sp.dma_start(bv_row[:, :], bv.rearrange("(a d) -> a d", a=1)).then_inc(bv_in, 16)
            for g in range(2, GROUPS):
                h = g % 2 * 4
                sp.dma_start(x[:, 4 * g:4 * g + 4, :], x_v[:, g // 2, h:h + 4, :]).then_inc(x_ld[g], 16)
            for i, w in enumerate((up_w, down_w)):
                sp.dma_start(raw[:, i, 0:16].rearrange("p (t n) -> p t n", t=2),
                             bass.AP(tensor=w.tensor, offset=w.offset,
                                     ap=[[8, P], [2 * HID, 2], [1, 8]])).then_inc(raw_in[i], 16)
                for t in range(2, NS):
                    at, n = region(t)
                    src = bass.AP(tensor=w.tensor, offset=w.offset + t * HID * 2,
                                  ap=[[n, 2 ** (8 - t)], [0, 2 ** (t - 1)], [1, n]])
                    sp.dma_start(raw[:, i, at:at + n], src).then_inc(raw_in[i], 16)
                if i == 0:
                    sp.dma_start(wexp_s[:, :], W_exp).then_inc(ffn_in, 16)
            sp.dma_start(wcon_s[:, :, :], W_con.rearrange("(c p) d -> p c d", p=P)).then_inc(ffn_in, 16)
            sp.dma_start(bexp_s[:, :], b_exp.rearrange("(p c) -> p c", c=CH)).then_inc(ffn_in, 16)
            for i, v in enumerate((b_con, down_bias)):
                sp.dma_start(fb_row[:, i:i + 1], v.rearrange("(d a) -> d a", a=1)).then_inc(ffn_in, 16)
            for dst, v in ((gamma_rep, gamma), (beta_rep, beta)):
                sp.dma_start(dst[:, :], bass.AP(tensor=v.tensor, offset=v.offset,
                                                ap=[[0, P], [1, D]])).then_inc(reps_in, 16)

            def store(b, k):
                g = 2 * b + k
                sp.wait_ge(out_ready, g + 1)
                sp.dma_start(out_v[:, bass.ds(b, 1), 4 * k:4 * k + 4, :].squeeze(1),
                             tiles(x, g)).then_inc(stored, 16)

            with sp.Fori(0, B) as b:
                store(b, 0)
                store(b, 1)
            sp.wait_ge(stored, 16 * GROUPS)

        @block.gpsimd
        def _(pool):
            pool.memset(ident[:, :], 0.0).then_inc(id_zero, 1)
            pool.wait_ge(id_zero, 1)
            pool.affine_select(out=ident[:, :], in_=ident[:, :], compare_op=ALU.not_equal, fill=1.0, base=0,
                               pattern=[[-1, P]], channel_multiplier=1).then_inc(id_ready, 1)
            pool.memset(power[:, :], -0.5).then_inc(power_ready, 1)
            pool.memset(eps1[:, :], LN_EPS).then_inc(power_ready, 1)
            pool.memset(eps23[:, 0:4], ATTN_LN_EPS).then_inc(power_ready, 1)
            pool.memset(eps23[:, 4:8], LN_EPS).then_inc(power_ready, 1)
            pool.memset(ones[:, :], 1.0).then_inc(const_ready, 1)
            pool.memset(ones_bf[:, :], 1.0).then_inc(const_ready, 1)
            pool.memset(r[:, :, D:D + 1], 1.0).then_inc(const_ready, 1)

            def ln1(b):
                s = slice(8 * b, 8 * b + 8)
                pool.wait_ge(ln1_stats, 2 * b + 2)
                pool.tensor_tensor(ve1[:, s], mv1[:, s, 1], eps1[:, :], ALU.add).then_inc(ln1_pool, 1)
                pool.tensor_scalar(nm1[:, s], mv1[:, s, 0], -1.0, None, ALU.mult).then_inc(ln1_pool, 1)
                pool.wait_ge(ln1_pool, 3 * b + 2)
                pool.tensor_tensor(rs1[:, s], ve1[:, s], power[:, :], ALU.pow).then_inc(ln1_pool, 1)
                pool.wait_ge(ln1_pool, 3 * b + 3)
                pool.tensor_tensor(nb1[:, s], nm1[:, s], rs1[:, s], ALU.mult).then_inc(ln1_scale, 1)

            pool.wait_ge(power_ready, 4)
            ln1(0)
            pool.memset(head_mask[:, :], 1.0).then_inc(mask_step, 1)
            hm = head_mask[:, :].rearrange("p (h e) -> p h e", e=HD)
            pool.wait_ge(mask_step, 1)
            pool.affine_select(out=hm, in_=hm, compare_op=ALU.is_ge, fill=0.0, base=0,
                               pattern=[[-HD, HEADS], [0, HD]], channel_multiplier=1).then_inc(mask_step, 1)
            pool.wait_ge(mask_step, 2)
            pool.affine_select(out=hm, in_=hm, compare_op=ALU.is_ge, fill=0.0, base=HD - 1,
                               pattern=[[HD, HEADS], [0, HD]], channel_multiplier=-1).then_inc(mask_step, 1)

            pool.wait_ge(rep_copied, 1)

            def scale_r(b, k):
                g = 2 * b + k
                pool.wait_ge(n1a_ready, g + 1)
                pool.wait_ge(n1v_ready, g + 1)
                apart(pool)
                pool.tensor_tensor(tiles(r, g), n1[:, k, :, :], per_tile(scale_rep, b), ALU.mult).then_inc(r_ready, 1)

            scale_r(0, 0)
            scale_r(0, 1)
            ln1(1)
            ln1(2)
            scale_r(1, 0)
            scale_r(1, 1)
            ln1(3)
            with pool.Fori(2, B) as b:
                scale_r(b, 0)
                scale_r(b, 1)
            pool.wait_ge(gate_ready, 1)
            pool.wait_ge(reps_in, 32)
            for b in range(B):
                pool.tensor_tensor(gg_rep[:, b, :], ga_rep[:, b, :], gamma_rep[:, :], ALU.mult).then_inc(gate_step, 1)
                pool.tensor_tensor(gbeta_rep[:, b, :], ga_rep[:, b, :], beta_rep[:, :], ALU.mult).then_inc(gate_step, 1)
            pool.wait_ge(raw_in[1], 16 * (NS - 1))
            products(pool, 1, range(NS))

            def divisor(b, k):
                g = 2 * b + k
                used(pool, den_ready, g)
                apart(pool)
                pool.tensor_tensor(qk[:, :, :], tiles(q, g), per_tile(ks_rep, b), ALU.mult).then_inc(qks_ready, 1)

            def step_b(b, k, attn=True, prev=True, more=True):
                g = 2 * b + k
                if prev:
                    normed_gate(b - 1 + k, 1 - k)
                if more:
                    if k == 0:
                        divisor(b, 1)
                    else:
                        divisor(b + 1, 0)
                if attn:
                    add_beta(b, k)
                scales(b, k, attn, prev)

            def normed_gate(b, k):
                pool.wait_ge(nh_ready, 2 * b + k + 1)
                apart(pool)
                pool.tensor_tensor(nh[:, k, :, :], nh[:, k, :, :], per_tile(gg_rep, b), ALU.mult).then_inc(nhg_ready, 1)

            def add_beta(b, k):
                g = 2 * b + k
                pool.tensor_tensor(tiles(x, g), tiles(x, g), per_tile(gbeta_rep, b), ALU.add).then_inc(xb_ready, 1)

            def scales(b, k, attn, prev):
                g = 2 * b + k
                lo, hi = (0 if attn else 4), (8 if prev else 4)
                if attn:
                    pool.wait_ge(ln2_stats, g + 1)
                if prev:
                    pool.wait_ge(ln3_stats, g)
                    used(pool, n3a_ready, g - 1)
                    used(pool, n3v_ready, g - 1)
                used(pool, nh_ready, g - 1)
                pool.tensor_tensor(ve[:, lo:hi], mv[:, k, lo:hi, 1], eps23[:, lo:hi], ALU.add).then_inc(ln_pool, 1)
                pool.tensor_scalar(nm[:, lo:hi], mv[:, k, lo:hi, 0], -1.0, None, ALU.mult).then_inc(ln_pool, 1)
                pool.wait_ge(ln_pool, 3 * g + 2)
                pool.tensor_tensor(rs[:, k, lo:hi], ve[:, lo:hi], power[:, lo:hi], ALU.pow).then_inc(ln_pool, 1)
                pool.wait_ge(ln_pool, 3 * g + 3)
                pool.tensor_tensor(nb[:, k, lo:hi], nm[:, lo:hi], rs[:, k, lo:hi], ALU.mult).then_inc(ln_scale, 1)

            pool.wait_ge(ksrep_saved, 1)
            divisor(0, 0)
            divisor(0, 1)
            pool.wait_ge(gate_step, 3 + 2 * B)
            add_beta(0, 0)
            divisor(1, 0)
            scales(0, 0, True, False)
            add_beta(0, 1)
            normed_gate(0, 0)

            def gate_w_down(b):
                apart(pool)
                pool.tensor_tensor(w_down_g[:, bass.ds(b, 1), :, :].squeeze(1), w_down[:, :, :],
                                   bc(gb_rep[:, bass.ds(b, 1), :], [P, CH, D]), ALU.mult).then_inc(wdg_ready, 1)

            scales(0, 1, True, True)
            divisor(1, 1)
            pool.wait_ge(gb_ready, 1)
            pool.wait_ge(wdown_saved, 1)
            gate_w_down(0)
            normed_gate(0, 1)
            add_beta(1, 0)
            pool.wait_ge(ln2_stats, 3)
            pool.wait_ge(nh_ready, 1)
            pool.tensor_tensor(ve[:, 0:4], mv[:, 0, 0:4, 1], eps23[:, 0:4], ALU.add).then_inc(ahead_step, 1)
            pool.tensor_scalar(nm[:, 0:4], mv[:, 0, 0:4, 0], -1.0, None, ALU.mult).then_inc(ahead_step, 1)
            pool.wait_ge(ahead_step, 2)
            pool.tensor_tensor(rs[:, 0, 0:4], ve[:, 0:4], power[:, 0:4], ALU.pow).then_inc(ahead_step, 1)
            pool.wait_ge(ahead_step, 3)
            pool.tensor_tensor(nb[:, 0, 0:4], nm[:, 0:4], rs[:, 0, 0:4], ALU.mult).then_inc(ahead_scale, 1)
            scales(1, 0, False, True)
            gate_w_down(1)
            step_b(1, 1)
            gate_w_down(2)
            with pool.Fori(2, B - 1) as b:
                step_b(b, 0)
                gate_w_down(b + 1)
                step_b(b, 1)
            step_b(B - 1, 0)
            step_b(B - 1, 1, more=False)
            step_b(B, 0, attn=False, more=False)

        @block.scalar
        def _(sc_e):
            sc_e.dma_start(c4[:, :], c_in).then_inc(c_ld, 16)
            sc_e.dma_start(wmod_s[:, :], wmod).then_inc(wmod_in, 16)
            sc_e.preload_act_table(ACT.Exp)
            sc_e.wait_ge(cT_ready, 1)
            sc_e.activation(sig[:, 0, :], bank[0][:, 0:B], ACT.Exp, scale=-1.0).then_inc(silu_exp, 1)
            for i, w in enumerate((Wq, Wk, Wv, Wd)):
                sc_e.dma_start(w_raw[:, i, :], w).then_inc(w_in, 16)
            sc_e.wait_ge(wT_ready, 1)
            sc_e.copy(wT[:, :, :], bank[1][:, :].rearrange("p (a b) -> p a b", a=4)).then_inc(wT_copied, 1)

            def norm1(b, k):
                g = 2 * b + k
                sc_e.wait_ge(ln1_scale, b + 1)
                used(sc_e, n1T_ready, g - 1)
                used(sc_e, r_ready, g - 1)
                apart(sc_e)
                for t in range(2):
                    s = g * TILES + t
                    ins = sc_e.activation(n1[:, k, t, :], x[:, bass.ds(s, 1), :].squeeze(1), ACT.Identity,
                                          bias=nb1[:, bass.ds(s, 1)], scale=rs1[:, bass.ds(s, 1)])
                ins.then_inc(n1a_ready, 1)

            def shift_scale(b, k):
                g = 2 * b + k
                sc_e.wait_ge(n1T_ready, g + 1)
                used(sc_e, qk_ready, 2 * (g - 1))
                apart(sc_e)
                sc_e.activation(hT[:, k, :], bank[k][:, :], ACT.Identity, bias=modc[:, 0, bass.ds(b, 1)],
                                scale=modc[:, 1, bass.ds(b, 1)]).then_inc(hT_ready, 1)

            def exps(b, k):
                g = 2 * b + k
                for h in range(2):
                    sc_e.wait_ge(qk_ready, 2 * g + h + 1)
                    used(sc_e, phi_ready, 2 * (g - 1) + h + 1)
                    sc_e.activation(ev[:, h, :], bank[2 + 2 * k + h][:, :], ACT.Relu, bias=1.0,
                                    scale=-1.0).then_inc(relu_ready, 1)
                for h in range(2):
                    sc_e.wait_ge(relu_ready, 2 * g + h + 1)
                    sc_e.activation(e[:, h, :], ev[:, h, :], ACT.Exp, scale=-1.0).then_inc(exp_ready, 1)

            def step_a(b, k, norm=True):
                g = 2 * b + k
                shift_scale(b, k)
                if norm:
                    norm1(b + 1, k)
                if not isinstance(b, int) or g > 0:
                    exps(b - 1 + k, 1 - k)

            norm1(0, 0)
            norm1(0, 1)
            sc_e.wait_ge(modc_ready, 1)
            shift_scale(0, 0)
            shift_scale(0, 1)
            sc_e.wait_ge(gates_mm, 1)
            sc_e.copy(ga_rep[:, :, :], bank[7][:, :].rearrange("p (a b) -> p a b", a=B)).then_inc(ga_copied, 1)
            exps(0, 0)
            norm1(1, 0)
            norm1(1, 1)
            with sc_e.Fori(1, B - 1) as b:
                step_a(b, 0)
                step_a(b, 1)
            step_a(B - 1, 0, norm=False)
            step_a(B - 1, 1, norm=False)
            exps(B - 1, 1)
            sc_e.wait_ge(wexpT_mm, 1)
            sc_e.copy(wexpT[:, :, :], bank[7][:, :].rearrange("p (a b) -> p a b", a=CH)).then_inc(wexpT_saved, 1)
            sc_e.preload_act_table(ACT.Gelu)

            def save_t_down(ic):
                sc_e.wait_ge(td_mm, ic + 1)
                sc_e.copy(t_down[:, ic, :].rearrange("q (p c) -> q c p", c=CH),
                          bank[7 - ic % 2][:, :].rearrange("q (c p) -> q c p", c=CH)).then_inc(td_saved, 1)

            sc_e.wait_ge(gT_mm, 1)
            sc_e.copy(gT[:, :, :], bank[2][:, :].rearrange("p (a b) -> p a b", a=B)).then_inc(gT_saved, 1)
            sc_e.wait_ge(ks_mm, 1)
            sc_e.copy(ks_row[:, :, :], bank[3][0:1, :].rearrange("p (a b) -> p a b", a=B)).then_inc(ks_saved, 1)
            sc_e.wait_ge(ksrep_mm, 1)
            sc_e.copy(ks_rep[:, :, :], bank[4][:, :].rearrange("p (a b) -> p a b", a=B)).then_inc(ksrep_saved, 1)
            sc_e.wait_ge(sh_mm, 1)
            sc_e.copy(sh3[:, :, :], bank[6][0:3, :].rearrange("p (a b) -> p a b", a=B)).then_inc(sh_ready, 1)
            sc_e.wait_ge(gb_mm, 1)
            sc_e.copy(gb_rep[:, :, :], bank[3][:, :].rearrange("p (a b) -> p a b", a=B)).then_inc(gb_ready, 1)
            sc_e.wait_ge(m_mm, 1)
            sc_e.copy(m_mat[:, :, :], bank[2][:, :].rearrange("p (a b) -> p a b", a=B)).then_inc(m_saved, 1)
            sc_e.wait_ge(fb_mm, 1)
            sc_e.copy(fb3[:, :, :], bank[4][0:3, :].rearrange("p (a b) -> p a b", a=B)).then_inc(fb_ready, 1)

            def attn_T(b, k):
                g = 2 * b + k
                sc_e.wait_ge(qnT_mm, g + 1)
                used(sc_e, attn_mm, g - 1)
                sc_e.copy(qT[:, k, :], bank[0][:, :]).then_inc(qT_ready, 1)

            def norm2(b, k, ahead=False):
                g = 2 * b + k
                if ahead:
                    sc_e.wait_ge(ahead_scale, 1)
                else:
                    sc_e.wait_ge(ln_scale, g + 1)
                used(sc_e, x1_ready, g - 1)
                for t in range(TILES):
                    ins = sc_e.activation(nh[:, k, t, :], hs[:, k, t, :], ACT.Identity,
                                          bias=nb[:, k, t:t + 1], scale=rs[:, k, t:t + 1])
                ins.then_inc(nh_ready, 1)

            def ffn_in_T(b, k):
                g = 2 * b + k
                sc_e.wait_ge(n3T_mm, g + 1)
                used(sc_e, up_mm, CH * (g - 1))
                apart(sc_e)
                sc_e.activation(h3T[:, k, :], bank[2][:, :], ACT.Identity, bias=modc[:, 3, bass.ds(b, 1)],
                                scale=modc[:, 4, bass.ds(b, 1)]).then_inc(h3T_ready, 1)

            def gelu(b, k, c):
                g = 2 * b + k
                sc_e.wait_ge(up_mm, CH * g + c + 1)
                if c == 0:
                    used(sc_e, down_mm, g - 1)
                sc_e.activation(act[:, k, c, :], bank[3 + c % 3][:, :], ACT.Gelu,
                                bias=b_up[:, c:c + 1]).then_inc(gelu_done, 1)

            def norm3(b, k):
                g = 2 * b + k
                sc_e.wait_ge(ln_scale, g + 1)
                used(sc_e, n3T_mm, g - 2)
                apart(sc_e)
                for t in range(2):
                    ins = sc_e.activation(n3[:, 1 - k, t, :], x[:, bass.ds(TILES * (g - 1) + t, 1), :].squeeze(1),
                                          ACT.Identity, bias=nb[:, k, 4 + t:5 + t], scale=rs[:, k, 4 + t:5 + t])
                ins.then_inc(n3a_ready, 1)

            def step_b(b, k, attn=True, ffn=True, norm=True, more=True, first=False):
                if ffn and not first:
                    ffn_in_T(b - 1, k)
                if ffn:
                    for c in range(CH - 1):
                        gelu(b - 1, k, c)
                if more:
                    attn_T(b + k, 1 - k)
                if norm and not first:
                    norm3(b, k)
                if attn:
                    norm2(b, k, ahead=first)
                if norm and first:
                    norm3(b, k)
                if ffn:
                    gelu(b - 1, k, CH - 1)

            attn_T(0, 0)
            save_t_down(0)
            save_t_down(1)
            attn_T(0, 1)
            save_t_down(2)
            save_t_down(3)
            norm2(0, 0)
            sc_e.wait_ge(wup_mm, 1)
            sc_e.copy(w_up[:, :], bank[4][:, :]).then_inc(wup_saved, 1)
            sc_e.wait_ge(wdown_mm, 1)
            sc_e.copy(w_down[:, :, :], bank[3][:, :].rearrange("p (a b) -> p a b", a=CH)).then_inc(wdown_saved, 1)
            norm3(0, 1)
            attn_T(1, 0)
            norm2(0, 1)
            ffn_in_T(0, 0)
            sc_e.wait_ge(bup_saved, 1)
            step_b(1, 0, first=True)
            step_b(1, 1)
            with sc_e.Fori(2, B - 1) as b:
                step_b(b, 0)
                step_b(b, 1)
            step_b(B - 1, 0)
            step_b(B - 1, 1, more=False)
            step_b(B, 0, attn=False, more=False)
            step_b(B, 1, attn=False, norm=False, more=False)

        @block.vector
        def _(dve):
            def stats1(g):
                dve.wait_ge(x_ld[g], 16)
                used(dve, ln1_stats, g - 1)
                for t in range(TILES):
                    ins = dve.bn_stats(bn1[:, g % 2, t, :], x[:, g * TILES + t, :])
                ins.then_inc(bn1_done, 1)
                dve.wait_ge(bn1_done, g + 1)
                for t in range(TILES):
                    ins = dve.bn_aggr(mv1[:, g * TILES + t, :], bn1[:, g % 2, t, :])
                ins.then_inc(ln1_stats, 1)

            dve.wait_ge(id_ready, 1)
            for t in range(SMALL):
                v = ident[:, :].rearrange("p (a i l) -> p a i l", i=2, l=2 ** t)[:, :, 1, :]
                ins = dve.reduce_sum(bits[:, t:t + 1], v, AX_XY)
            ins.then_inc(bits_step, 1)
            dve.wait_ge(bits_step, 1)
            dve.tensor_scalar(nbits[:, :], bits[:, :], -1.0, 1.0, ALU.mult, ALU.add).then_inc(bits_step, 1)
            stats1(0)
            dve.wait_ge(silu_exp, 1)
            dve.tensor_scalar(sig[:, 1, :], sig[:, 0, :], 1.0, None, ALU.add).then_inc(silu_step, 1)
            dve.wait_ge(silu_step, 1)
            dve.reciprocal(sig[:, 2, :], sig[:, 1, :]).then_inc(silu_step, 1)
            dve.wait_ge(silu_step, 2)
            dve.tensor_tensor(sc[:, :], bank[0][:, 0:B], sig[:, 2, :], ALU.mult).then_inc(sc_ready, 1)
            dve.wait_ge(sc_ready, 1)
            dve.tensor_copy(sc_rep[:, :, :], bc(sc[:, :].unsqueeze(2), [P, B, P])).then_inc(sc_rep_ready, 1)
            stats1(1)
            dve.wait_ge(modT_ready, 1)
            dve.tensor_copy(modc[:, :, :], bank[5][:, 0:24].rearrange("p (j b) -> p j b", j=6)).then_inc(modc_step, 1)
            dve.wait_ge(modc_step, 1)
            for j in (1, 4):
                ins = dve.tensor_scalar(modc[:, j, :], modc[:, j, :], 1.0, None, ALU.add)
            ins.then_inc(modc_ready, 1)
            dve.wait_ge(cols_ready, 1)
            dve.tensor_copy(cols[:, :], bank[3][:, 0:7]).then_inc(cols_copied, 1)
            dve.wait_ge(cols_copied, 1)
            dve.wait_ge(modc_step, 1)
            dve.tensor_scalar(bias_1[:, 0:2], cols[:, 0:2], 1.0, None, ALU.add)
            dve.tensor_scalar(bias_1[:, 2:], modc[:, 0, :], cols[:, 2:3], None, ALU.add).then_inc(bias_step, 1)
            dve.wait_ge(bias_step, 1)
            dve.tensor_copy(bias_h[:, 0, :], bias_1[:, :]).then_inc(bias_step, 1)
            dve.wait_ge(bias_step, 2)
            dve.tensor_copy(bias_p[:, :, 0], bias_h[:, 0, :])
            dve.tensor_tensor(bias_f[:, :], bias_1[:, :], bias_h[:, 0, :], ALU.subtract).then_inc(bias_step, 1)
            dve.wait_ge(bias_step, 3)
            dve.tensor_copy(bias_h[:, 1, :], bias_f[:, :]).then_inc(bias_step, 1)
            dve.wait_ge(bias_step, 4)
            dve.tensor_copy(bias_p[:, :, 1], bias_h[:, 1, :])
            dve.tensor_tensor(bias_p[:, :, 2], bias_f[:, :], bias_h[:, 1, :], ALU.subtract).then_inc(bias_step, 1)

            def norm1(b, k):
                g = 2 * b + k
                dve.wait_ge(ln1_scale, b + 1)
                used(dve, n1T_ready, g - 1)
                used(dve, r_ready, g - 1)
                apart(dve)
                for t in range(2, TILES):
                    s = g * TILES + t
                    ins = dve.tensor_scalar(n1[:, k, t, :], x[:, bass.ds(s, 1), :].squeeze(1),
                                            rs1[:, bass.ds(s, 1)], nb1[:, bass.ds(s, 1)], ALU.mult, ALU.add)
                ins.then_inc(n1v_ready, 1)

            norm1(0, 0)
            norm1(0, 1)
            dve.wait_ge(mod_rep, 1)
            dve.tensor_scalar(scale_rep[:, :, :], bank[6][:, :].rearrange("p (a b) -> p a b", a=B), 1.0, None,
                              ALU.add).then_inc(rep_copied, 1)
            dve.nop().then_inc(g_saved, 1)
            stats1(2)
            stats1(3)
            dve.wait_ge(parts_mm, 1)
            dve.tensor_copy(bias3[:, :], bank[4][0:3, 0:2 * D]).then_inc(bias_ready, 1)
            stats1(4)
            stats1(5)

            def weights(i, t, bit):
                at, n = region(t)
                return raw[:, bass.ds(i, 1), at:at + n].squeeze(1).rearrange("p (l o i) -> p i o l", o=2, i=2)[:, bit]

            def chosen(i, t):
                return fsel[:, bass.ds(i, 1), 2 ** (t + 1):2 ** (t + 2)].squeeze(1).rearrange("p (o l) -> p o l", o=2)

            def select_clear(i):
                for t in range(2, NS):
                    ins = dve.tensor_scalar(chosen(i, t), weights(i, t, 0), nbits[:, t - 2:t - 1], None, ALU.mult)
                ins.then_inc(fsel_step, 1)

            def select_set(i):
                dve.wait_ge(fsel_step, 2 * i + 1)
                apart(dve)
                for t in range(2, NS):
                    ins = dve.scalar_tensor_tensor(out=chosen(i, t), in0=weights(i, t, 1), scalar=bits[:, t - 2:t - 1],
                                                   in1=chosen(i, t), op0=ALU.mult, op1=ALU.add)
                ins.then_inc(fsel_step, 1)

            def phi(b, k):
                g = 2 * b + k
                dve.wait_ge(sums_done, g + 1)
                for h in range(2):
                    dve.wait_ge(exp_ready, 2 * g + h + 1)
                    em = e[:, h, :].rearrange("p (t w d) -> p t w d", t=2, w=2)
                    pv = bank[2 + 2 * k + h][:, :].rearrange("p (t w d) -> p t w d", t=2, w=2)
                    dve.tensor_tensor(kf[:, k, 2 * h:2 * h + 2, :], em[:, :, 1, :], pv[:, :, 1, :], ALU.max)
                    dve.tensor_tensor(q[:, bass.ds(TILES * g + 2 * h, 2), :], em[:, :, 0, :], pv[:, :, 0, :],
                                      ALU.max).then_inc(phi_ready, 1)

            def save_g(b):
                dve.wait_ge(sums_done, 2 * b + 4)
                dve.tensor_copy(gs[:, bass.ds(b, 1), :].squeeze(1), bank[6][:, 0:D + 1]).then_inc(g_saved, 1)

            def step_a(b, k, norm=True):
                g = 2 * b + k
                if norm:
                    norm1(b + 1, k)
                if not isinstance(b, int) or g > 0:
                    phi(b - 1 + k, 1 - k)

            norm1(1, 0)
            dve.wait_ge(ga_copied, 1)
            dve.tensor_scalar(ga_sign[:, :, :], ga_rep[:, :, :], 0.0, 2.0, ALU.is_ge, ALU.mult).then_inc(gate_step, 1)
            dve.scalar_tensor_tensor(out=ga_abs[:, :, :], in0=ga_rep[:, :, :], scalar=-1.0, in1=ga_rep[:, :, :],
                                     op0=ALU.mult, op1=ALU.max).then_inc(gate_step, 1)
            dve.wait_ge(gate_step, 2)
            dve.tensor_scalar(ga_abs[:, :, :], ga_abs[:, :, :], GATE_FLOOR, None, ALU.max).then_inc(gate_step, 1)
            dve.wait_ge(gate_step, 3)
            dve.scalar_tensor_tensor(out=ga_rep[:, :, :], in0=ga_sign[:, :, :], scalar=-1.0, in1=ga_abs[:, :, :],
                                     op0=ALU.add, op1=ALU.mult).then_inc(gate_ready, 1)
            phi(0, 0)
            norm1(1, 1)
            stats1(6)
            stats1(7)
            for i in range(2):
                dve.wait_ge(raw_in[i], 16 * (NS - 1))
            with dve.Fori(1, B - 1) as b:
                step_a(b, 0)
                select_clear(b - 1)
                step_a(b, 1)
                select_set(b - 1)
                save_g(b - 1)
            step_a(B - 1, 0, norm=False)
            dve.wait_ge(vb_mm, 1)
            dve.wait_ge(bv_in, 16)
            dve.tensor_tensor(vb_row[:, :, :], bank[7][0:1, :].rearrange("p (a b) -> p a b", a=B),
                              bc(bv_row[:, :].unsqueeze(1), [1, B, D]), ALU.add).then_inc(vb_ready, 1)
            products(dve, 0, range(NS - 2))
            step_a(B - 1, 1, norm=False)
            save_g(B - 2)
            products(dve, 0, (NS - 2,))
            phi(B - 1, 1)
            dve.wait_ge(ffn_in, 80)
            dve.tensor_tensor(bsum[:, :], fb_row[:, 0:1], fb_row[:, 1:2], ALU.add).then_inc(gate_b, 1)
            dve.tensor_scalar(gbw[:, 0, :], modc[:, 5, :], 0.0, 2.0, ALU.is_ge, ALU.mult).then_inc(gate_b, 1)
            dve.scalar_tensor_tensor(out=gbw[:, 1, :], in0=modc[:, 5, :], scalar=-1.0, in1=modc[:, 5, :],
                                     op0=ALU.mult, op1=ALU.max).then_inc(gate_b, 1)
            dve.wait_ge(gate_b, 3)
            dve.tensor_scalar(gbw[:, 2, :], gbw[:, 1, :], GATE_FLOOR, None, ALU.max).then_inc(gate_b, 1)
            dve.wait_ge(gate_b, 4)
            dve.scalar_tensor_tensor(out=gbc[:, 0, :], in0=gbw[:, 0, :], scalar=-1.0, in1=gbw[:, 2, :],
                                     op0=ALU.add, op1=ALU.mult).then_inc(gate_b, 1)
            dve.wait_ge(gate_b, 5)
            dve.tensor_scalar(gbc[:, 1, :], gbc[:, 0, :], bsum[:, 0:1], None, ALU.mult).then_inc(gate_b, 1)
            for b in range(B):
                ins = dve.tensor_scalar(gb_diag[:, b, :], ident[:, :], gbc[:, 0, b:b + 1], None, ALU.mult)
            ins.then_inc(gb_diag_ready, 1)
            save_g(B - 1)

            dve.wait_ge(g_saved, B + 1)
            dve.tensor_scalar(ks_eps[:, :], gs[:, :, D], ATTN_EPS, None, ALU.add).then_inc(ks_eps_ready, 1)
            dve.wait_ge(ks_eps_ready, 1)
            for b in range(B):
                ins = dve.tensor_scalar(ks_diag[:, b, :], ident[:, :], ks_eps[:, b:b + 1], None, ALU.mult)
            ins.then_inc(ks_diag_ready, 1)
            dve.wait_ge(gate_b, 6)
            dve.tensor_copy(fb_h[:, 0, :], gbc[:, 1, :]).then_inc(fb_step, 1)
            dve.wait_ge(fb_step, 1)
            dve.tensor_copy(fb_p[:, :, 0], fb_h[:, 0, :])
            dve.tensor_tensor(fb_f[:, :], gbc[:, 1, :], fb_h[:, 0, :], ALU.subtract).then_inc(fb_step, 1)
            dve.wait_ge(fb_step, 2)
            dve.tensor_copy(fb_h[:, 1, :], fb_f[:, :]).then_inc(fb_step, 1)
            dve.wait_ge(fb_step, 3)
            dve.tensor_copy(fb_p[:, :, 1], fb_h[:, 1, :])
            dve.tensor_tensor(fb_p[:, :, 2], fb_f[:, :], fb_h[:, 1, :], ALU.subtract).then_inc(fb_step, 1)
            products(dve, 0, (NS - 1,))
            dve.wait_ge(kv_mm, 1)
            dve.wait_ge(mask_step, 3)
            dve.tensor_tensor(kvT[:, :, :], bank[5][:, :].rearrange("p (a b) -> p a b", a=B),
                              bc(head_mask[:, :].unsqueeze(1), [P, B, P]), ALU.mult).then_inc(kv_saved, 1)

            def divide(b, k):
                g = 2 * b + k
                dve.wait_ge(qks_ready, g + 1)
                used(dve, z_ready, g)
                dve.reduce_sum(den[:, :], qk[:, :, :].rearrange("p t (h e) -> p (t h) e", e=HD), AX_X).then_inc(den_ready, 1)
                dve.wait_ge(den_ready, g + 1)
                used(dve, qn_ready, g)
                dve.reciprocal(z[:, :], den[:, :]).then_inc(z_ready, 1)
                dve.wait_ge(z_ready, g + 1)
                used(dve, qnT_mm, g - 1)
                dve.tensor_tensor(qn[:, k, :, :].rearrange("p t (h e) -> p (t h) e", e=HD),
                                  tiles(q, g).rearrange("p t (h e) -> p (t h) e", e=HD),
                                  bc(z[:, :].unsqueeze(2), [P, TILES * HEADS, HD]), ALU.mult).then_inc(qn_ready, 1)

            def attention_out(b, k):
                g = 2 * b + k
                dve.wait_ge(attn_mm, g + 1)
                dve.wait_ge(r_ready, g + 1)
                used(dve, nh_ready, g - 1)
                dve.tensor_tensor(hs[:, k, :, :], bank[1][:, :].rearrange("p (t d) -> p t d", t=TILES),
                                  tiles(r, g), ALU.add).then_inc(hs_ready, 1)
                dve.wait_ge(hs_ready, g + 1)
                used(dve, ln2_stats, g)
                for t in range(TILES):
                    ins = dve.bn_stats(bn2[:, t, :], hs[:, k, t, :])
                ins.then_inc(bn2_done, 1)
                dve.wait_ge(bn2_done, g + 1)
                for t in range(TILES):
                    ins = dve.bn_aggr(mv[:, k, t, :], bn2[:, t, :])
                ins.then_inc(ln2_stats, 1)

            def step_b(b, k, attn=True, prev=True, more=True, final=True, norm=True):
                g = 2 * b + k
                if attn:
                    attention_out(b, k)
                if prev:
                    dve.wait_ge(nhg_ready, g)
                    dve.wait_ge(xb_ready, g)
                    dve.tensor_tensor(tiles(x, g - 1), nh[:, 1 - k, :, :], tiles(x, g - 1), ALU.add).then_inc(x1_ready, 1)
                    dve.wait_ge(x1_ready, g)
                    used(dve, ln3_stats, g - 1)
                    for t in range(TILES):
                        ins = dve.bn_stats(bn3[:, t, :], x[:, bass.ds(TILES * (g - 1) + t, 1), :].squeeze(1))
                    ins.then_inc(bn3_done, 1)
                    dve.wait_ge(bn3_done, g)
                    for t in range(TILES):
                        ins = dve.bn_aggr(mv[:, k, 4 + t, :], bn3[:, t, :])
                    ins.then_inc(ln3_stats, 1)
                if more:
                    if k == 0:
                        divide(b, 1)
                    else:
                        divide(b + 1, 0)
                if final:
                    dve.wait_ge(down_mm, g - 2)
                    dve.tensor_tensor(tiles(x, g - 3), bank[7 - k][:, :].rearrange("p (t d) -> p t d", t=TILES),
                                      tiles(x, g - 3), ALU.add).then_inc(out_ready, 1)
                if norm:
                    dve.wait_ge(ln_scale, g + 1)
                    used(dve, n3T_mm, g - 2)
                    apart(dve)
                    for t in range(2, TILES):
                        ins = dve.tensor_scalar(n3[:, 1 - k, t, :], x[:, bass.ds(TILES * (g - 1) + t, 1), :].squeeze(1),
                                                rs[:, k, 4 + t:5 + t], nb[:, k, 4 + t:5 + t], ALU.mult, ALU.add)
                    ins.then_inc(n3v_ready, 1)

            divide(0, 0)
            divide(0, 1)
            attention_out(0, 0)
            attention_out(0, 1)
            step_b(0, 1, attn=False, final=False)
            divide(1, 1)
            dve.wait_ge(bup_mm, 1)
            dve.tensor_tensor(b_up[:, :], bank[5][:, 0:CH], cols[:, 3:7], ALU.add).then_inc(bup_saved, 1)
            step_b(1, 0, more=False, final=False)
            step_b(1, 1)
            with dve.Fori(2, B - 1) as b:
                step_b(b, 0)
                step_b(b, 1)
            step_b(B - 1, 0)
            step_b(B - 1, 1, more=False)
            step_b(B, 0, attn=False, more=False)
            step_b(B, 1, attn=False, prev=False, more=False, norm=False)
            step_b(B + 1, 0, attn=False, prev=False, more=False, norm=False)

        @block.tensor
        def _(pe):
            pe.wait_ge(id_ready, 1)
            pe.wait_ge(c_ld, 16)
            pe.transpose(bank[0][:, 0:B], c4[:, :], ident[0:B, 0:B]).then_inc(cT_ready, 1)
            pe.wait_ge(wmod_in, 16)
            pe.wait_ge(sc_ready, 1)
            for j in range(6):
                ins = pe.matmul(bank[5][:, 4 * j:4 + 4 * j], wmod_s[:, j * D:(j + 1) * D], sc[:, :],
                                start=True, stop=True)
            ins.then_inc(modT_ready, 1)
            pe.wait_ge(rows_in, 64)
            pe.transpose(bank[3][:, 0:7], rows[:, :], ident[0:7, 0:7]).then_inc(cols_ready, 1)
            pe.wait_ge(w_in, 64)
            for i in range(4):
                ins = pe.transpose(bank[1][:, i * P:(i + 1) * P], w_raw[:, i, :], ident[:, :])
            ins.then_inc(wT_ready, 1)

            def replicate_mod(j, done):
                for b in range(B):
                    ins = pe.matmul(bank[5 + j][:, b * D:(b + 1) * D], sc_rep[:, b, :], wmod_s[:, j * D:(j + 1) * D],
                                    start=True, stop=True)
                ins.then_inc(done, 1)

            pe.wait_ge(sc_rep_ready, 1)
            replicate_mod(1, mod_rep)

            def transposes1(b, k):
                g = 2 * b + k
                pe.wait_ge(n1a_ready, g + 1)
                pe.wait_ge(n1v_ready, g + 1)
                used(pe, hT_ready, g - 1)
                for t in range(TILES):
                    ins = pe.transpose(bank[k][:, t * P:(t + 1) * P], n1[:, k, t, :], ident[:, :])
                ins.then_inc(n1T_ready, 1)

            def qk_product(b, k):
                g = 2 * b + k
                pe.wait_ge(hT_ready, g + 1)
                for t in range(TILES):
                    if t % 2 == 0:
                        used(pe, phi_ready, 2 * (g - 2) + t // 2 + 1)
                    o = bank[2 + 2 * k + t // 2][:, t % 2 * 256:t % 2 * 256 + 256]
                    pe.matmul(o, ones_bf[0:3, :], bias3[:, :], start=True, stop=False)
                    ins = pe.matmul(o, hT[:, k, t * P:(t + 1) * P], wT[:, 0:2, :], start=False, stop=True)
                    if t % 2:
                        ins.then_inc(qk_ready, 1)

            def sums(b, k):
                g = 2 * b + k
                pe.wait_ge(phi_ready, 2 * g + 2)
                pe.wait_ge(r_ready, g + 1)
                if k == 0:
                    pe.wait_ge(g_saved, b + 1)
                for t in range(TILES):
                    ins = pe.matmul(bank[6][:, 0:D + 1], kf[:, k, t, :], r[:, bass.ds(TILES * g + t, 1), :].squeeze(1),
                                    start=(k == 0 and t == 0), stop=(k == 1 and t == TILES - 1))
                ins.then_inc(sums_done, 1)

            def step_a(b, k):
                g = 2 * b + k
                transposes1(b + k, 1 - k)
                qk_product(b, k)
                if not isinstance(b, int) or b > 0:
                    sums(b - 1, k)

            transposes1(0, 0)
            pe.wait_ge(bias_step, 5)
            for w in range(2):
                ins = pe.transpose(bank[4][0:3, w * D:(w + 1) * D], bias_p[:, w, :], ident[:, :])
            ins.then_inc(parts_mm, 1)
            pe.wait_ge(wT_copied, 1)
            transposes1(0, 1)
            replicate_mod(2, gates_mm)
            pe.wait_ge(bias_ready, 1)
            pe.wait_ge(const_ready, 3)
            qk_product(0, 0)
            qk_product(0, 1)
            transposes1(1, 0)
            pe.nop().then_inc(sums_done, 2)
            with pe.Fori(1, B - 1) as b:
                step_a(b, 0)
                step_a(b, 1)
            pe.wait_ge(ga_copied, 1)
            pe.wait_ge(modc_ready, 1)
            for b in range(B):
                ins = pe.matmul(bank[7][0:1, b * D:(b + 1) * D], modc[:, 0, b:b + 1], wT[:, 2, :], start=True, stop=True)
            ins.then_inc(vb_mm, 1)
            step_a(B - 1, 0)
            qk_product(B - 1, 1)
            sums(B - 2, 1)
            sums(B - 1, 0)
            pe.wait_ge(ffn_in, 80)
            pe.wait_ge(vb_ready, 1)
            for c in range(CH):
                ins = pe.transpose(bank[7][:, c * P:(c + 1) * P],
                                   wexp_s[:, :].rearrange("d (p c) -> d c p", c=CH)[:, c], ident[:, :])
            ins.then_inc(wexpT_mm, 1)
            sums(B - 1, 1)

            def t_down_transposes(ic):
                if ic < 2:
                    pe.wait_ge(wexpT_saved, 1)
                    pe.wait_ge(sh_ready, 1)
                else:
                    pe.wait_ge(td_saved, ic - 1)
                for c in range(CH):
                    ins = pe.transpose(bank[7 - ic % 2][:, c * P:(c + 1) * P], t_mat[:, 1, c, ic * P:(ic + 1) * P],
                                       ident[:, :])
                ins.then_inc(td_mm, 1)

            pe.wait_ge(g_saved, B + 1)
            pe.wait_ge(phi_ready, 2 * GROUPS)
            for b in range(B):
                ins = pe.transpose(bank[2][:, b * P:(b + 1) * P], gs[:, b, 0:D], ident[:, :])
            ins.then_inc(gT_mm, 1)
            for b in range(B):
                ins = pe.matmul(bank[3][0:1, b * P:(b + 1) * P], gs[:, b, D:D + 1], ident[:, :], start=True, stop=True)
            ins.then_inc(ks_mm, 1)
            pe.wait_ge(ks_diag_ready, 1)
            pe.matmul(bank[4][:, :], ones[:, :], ks_diag[:, :, :], start=True, stop=True).then_inc(ksrep_mm, 1)
            pe.wait_ge(gT_saved, 1)
            pe.wait_ge(ks_saved, 1)
            for b in range(B):
                pe.matmul(bank[5][:, b * P:(b + 1) * P], wT[:, 2, :], gT[:, b, :], start=True, stop=False)
                ins = pe.matmul(bank[5][:, b * P:(b + 1) * P], vb_row[:, b, :], ks_row[:, b, :], start=False, stop=True)
            ins.then_inc(kv_mm, 1)
            for b in range(B):
                ins = pe.transpose(bank[6][0:3, b * P:(b + 1) * P], bias_p[:, 2 + b, :], ident[:, :])
            ins.then_inc(sh_mm, 1)
            pe.wait_ge(gb_diag_ready, 1)
            pe.matmul(bank[3][:, :], ones[:, :], gb_diag[:, :, :], start=True, stop=True).then_inc(gb_mm, 1)
            pe.wait_ge(kv_saved, 1)
            for b in range(B):
                ins = pe.matmul(bank[2][:, b * P:(b + 1) * P], kvT[:, b, :], wT[:, 3, :], start=True, stop=True)
            ins.then_inc(m_mm, 1)
            pe.wait_ge(fb_step, 4)
            pe.wait_ge(ksrep_saved, 1)
            for b in range(B):
                ins = pe.transpose(bank[4][0:3, b * P:(b + 1) * P], fb_p[:, b, :], ident[:, :])
            ins.then_inc(fb_mm, 1)
            def q_transposes(b, k):
                g = 2 * b + k
                pe.wait_ge(qn_ready, g + 1)
                used(pe, qT_ready, g)
                for t in range(TILES):
                    ins = pe.transpose(bank[0][:, t * P:(t + 1) * P], qn[:, k, t, :], ident[:, :])
                ins.then_inc(qnT_mm, 1)

            def attention(b, k):
                g = 2 * b + k
                used(pe, hs_ready, g)
                apart(pe)
                pe.matmul(bank[1][:, :], ones_bf[0:3, :], bc(sh3[:, bass.ds(b, 1), :], [3, TILES, D]),
                          start=True, stop=False, skip_group_check=True)
                pe.wait_ge(qT_ready, g + 1)
                for t in range(TILES):
                    ins = pe.matmul(bank[1][:, t * P:(t + 1) * P], qT[:, k, t * P:(t + 1) * P],
                                    m_mat[:, bass.ds(b, 1), :].squeeze(1), start=False, stop=True, skip_group_check=True)
                ins.then_inc(attn_mm, 1)

            def transposes3(b, k):
                g = 2 * b + k
                pe.wait_ge(n3a_ready, g + 1)
                pe.wait_ge(n3v_ready, g + 1)
                used(pe, h3T_ready, g)
                for t in range(TILES):
                    ins = pe.transpose(bank[2][:, t * P:(t + 1) * P], n3[:, k, t, :], ident[:, :])
                ins.then_inc(n3T_mm, 1)

            def up(b, k, c):
                g = 2 * b + k
                if c == 0:
                    pe.wait_ge(h3T_ready, g + 1)
                used(pe, gelu_done, CH * g + (0, -2, -1, 1)[c])
                pe.matmul(bank[3 + c % 3][:, :], w_up[:, c * P:(c + 1) * P], h3T[:, k, :],
                          start=True, stop=True).then_inc(up_mm, 1)

            def down(b, k, c):
                g = 2 * b + k
                if c == 0:
                    used(pe, out_ready, g - 1)
                    pe.wait_ge(wdg_ready, b + 1)
                    apart(pe)
                    pe.matmul(bank[6 + k][:, :], ones_bf[0:3, :], bc(fb3[:, bass.ds(b, 1), :], [3, TILES, D]),
                              start=True, stop=False, skip_group_check=True)
                pe.wait_ge(gelu_done, CH * g + c + 1)
                apart(pe)
                for t in range(TILES):
                    ins = pe.matmul(bank[6 + k][:, t * P:(t + 1) * P], act[:, k, c, t * P:(t + 1) * P],
                                    w_down_g[:, bass.ds(b, 1), c, :].squeeze(1), start=False, stop=(c == CH - 1),
                                    skip_group_check=True)
                if c == CH - 1:
                    ins.then_inc(down_mm, 1)

            def step_b(b, k, last=True, more=True):
                if last:
                    transposes3(b - 1, k)
                    down(b - 2 + k, 1 - k, 2)
                    down(b - 2 + k, 1 - k, 3)
                up(b - 1, k, 0)
                up(b - 1, k, 1)
                up(b - 1, k, 2)
                down(b - 1, k, 0)
                if more:
                    q_transposes(b + k, 1 - k)
                up(b - 1, k, 3)
                if more:
                    attention(b + k, 1 - k)
                down(b - 1, k, 1)

            def w_up_product(c):
                ins = pe.matmul(bank[4][:, :], wexpT[:, c, :], t_mat[:, 0, c, :], start=(c == 0), stop=(c == CH - 1))
                if c == CH - 1:
                    ins.then_inc(wup_mm, 1)

            def b_up_product(ic):
                for c in range(CH):
                    ins = pe.matmul(bank[5][:, ic:ic + 1], t_mat[:, 0, c, ic * P:(ic + 1) * P], bexp_s[:, c:c + 1],
                                    start=(c == 0), stop=(c == CH - 1))
                if ic == CH - 1:
                    ins.then_inc(bup_mm, 1)

            q_transposes(0, 0)
            pe.wait_ge(t_ready[1], 1)
            t_down_transposes(0)
            pe.wait_ge(m_saved, 1)
            attention(0, 0)
            t_down_transposes(1)
            pe.wait_ge(t_ready[0], 1)
            pe.wait_ge(fb_ready, 1)
            q_transposes(0, 1)
            t_down_transposes(2)
            w_up_product(0)
            t_down_transposes(3)
            attention(0, 1)
            for c in range(1, CH):
                w_up_product(c)
            pe.wait_ge(td_saved, CH)
            pe.wait_ge(gb_ready, 1)
            for c in range(CH):
                for ic in range(CH):
                    ins = pe.matmul(bank[3][:, c * P:(c + 1) * P], t_down[:, ic, c * P:(c + 1) * P], wcon_s[:, ic, :],
                                    start=(ic == 0), stop=(ic == CH - 1))
            ins.then_inc(wdown_mm, 1)
            b_up_product(0)
            b_up_product(1)
            q_transposes(1, 0)
            b_up_product(2)
            transposes3(0, 0)
            b_up_product(3)
            attention(1, 0)
            pe.wait_ge(wdown_saved, 1)
            pe.wait_ge(wup_saved, 1)
            pe.wait_ge(bup_saved, 1)
            step_b(1, 0, last=False)
            step_b(1, 1)
            with pe.Fori(2, B - 1) as b:
                step_b(b, 0)
                step_b(b, 1)
            step_b(B - 1, 0)
            step_b(B - 1, 1, more=False)
            step_b(B, 0, more=False)
            step_b(B, 1, more=False)
            down(B - 1, 1, 2)
            down(B - 1, 1, 3)


_INS = ['L0_attn_input_tensor', 'L0_attn_Wq', 'L0_attn_bq', 'L0_attn_Wk', 'L0_attn_bk', 'L0_attn_Wv', 'L0_attn_bv',
        'L0_attn_Wd', 'L0_attn_bd', 'L0_attn_gamma', 'L0_attn_beta', 'L0_ffn_W_exp', 'L0_ffn_b_exp',
        'L0_ffn_up_weights', 'L0_ffn_up_bias', 'L0_ffn_down_weights', 'L0_ffn_W_con', 'L0_ffn_b_con',
        'L0_ffn_down_bias', 'L0_c', 'L0_wmod']
_OUTS = [((4, 1024, 128), 'float32')]


def kernel(**inputs):
    import numpy as _np
    import concourse.bacc as _bacc
    from concourse import mybir as _mybir
    from concourse.bass_utils import run_bass_kernel_spmd as _run

    nc = _bacc.Bacc("TRN2", target_bir_lowering=False, num_devices=1)
    arrays, args = {}, []
    for name in _INS:
        a = _np.ascontiguousarray(inputs[name])
        arrays[f"in_{name}_dram"] = a
        args.append(nc.dram_tensor(f"in_{name}_dram", a.shape, _mybir.dt.from_np(a.dtype), kind="ExternalInput").ap())
    for i, (shape, dtype) in enumerate(_OUTS):
        dt = _mybir.dt.from_np(_np.dtype(dtype))
        args.append(nc.dram_tensor(f"out_{i}_dram", shape, dt, kind="ExternalOutput").ap())
    adaln_block_kernel(nc, *args)
    r = _run(nc, [arrays], core_ids=[0])
    got = tuple(r.results[0][f"out_{i}_dram"] for i in range(len(_OUTS)))
    return got[0]
```
